# Optimizing a Trainium2 kernel written in Bass

```python
import numpy as np
import jax
import jax.numpy as jnp

def _softmax(x, axis=-1):
    return jax.nn.softmax(x, axis=axis)

def _gelu(x):
    return jax.nn.gelu(x, approximate=True)

def _silu(x):
    return jax.nn.silu(x)

def _sigmoid(x):
    return jax.nn.sigmoid(x)

def _layernorm(x, axis=-1, eps=1e-05):
    m = jnp.mean(x, axis=axis, keepdims=True)
    v = jnp.var(x, axis=axis, keepdims=True)
    return (x - m) / jnp.sqrt(v + eps)

def _scatter_add(tgt, idx, src, axis=0):
    return tgt.at[idx].add(src)

def _segment_sum(src, seg, n):
    return jax.ops.segment_sum(src, seg, n)
kernel_name = 'mk_recurrent_d1_jaxref_r8_b58ba0'

def setup_inputs(seed: int=0):
    np.random.seed(seed)
    _w = jnp.asarray

    def _L0_attn_setup():
        import jax, jax.numpy as jnp
        import numpy as np
        EMBED_DIM = 256
        NUM_HEADS = 32
        HEAD_DIM = EMBED_DIM // NUM_HEADS
        BATCH = 2
        SEQ_LEN = 256
        key = jax.random.key(seed)
        ks = jax.random.split(key, 5)
        scale = 1.0 / np.sqrt(EMBED_DIM)
        x = jax.random.normal(ks[0], (BATCH, SEQ_LEN, EMBED_DIM), dtype=jnp.float32)
        Wq = jax.random.normal(ks[1], (EMBED_DIM, EMBED_DIM), dtype=jnp.float32) * scale
        Wk = jax.random.normal(ks[2], (EMBED_DIM, EMBED_DIM), dtype=jnp.float32) * scale
        Wv = jax.random.normal(ks[3], (EMBED_DIM, EMBED_DIM), dtype=jnp.float32) * scale
        Wo = jax.random.normal(ks[4], (EMBED_DIM, EMBED_DIM), dtype=jnp.float32) * scale
        return {'x': x, 'Wq': Wq, 'Wk': Wk, 'Wv': Wv, 'Wo': Wo}
    _L0_attn_in = _L0_attn_setup()

    def _L0_ffn_setup():
        import jax, jax.numpy as jnp
        import numpy as np
        N_GROUP = 8
        TOPK_GROUP = 3
        TOP_K = 6
        ROUTED_SCALE = 1.0
        key = jax.random.key(seed)
        ks = jax.random.split(key, 8)
        B, S, H, I, E = (2, 256, 256, 128, 32)
        SI = 2 * I
        s = 0.02
        return {'hidden_states': jax.random.normal(ks[0], (B, S, H), jnp.float32), 'gate_weight': jax.random.normal(ks[1], (E, H), jnp.float32) * s, 'w1': jax.random.normal(ks[2], (E, I, H), jnp.float32) * s, 'w2': jax.random.normal(ks[3], (E, H, I), jnp.float32) * s, 'w3': jax.random.normal(ks[4], (E, I, H), jnp.float32) * s, 'sw1': jax.random.normal(ks[5], (SI, H), jnp.float32) * s, 'sw2': jax.random.normal(ks[6], (H, SI), jnp.float32) * s, 'sw3': jax.random.normal(ks[7], (SI, H), jnp.float32) * s}
    _L0_ffn_in = _L0_ffn_setup()
    _d = {'L0_attn_x': _L0_attn_in['x'], 'L0_attn_Wq': _L0_attn_in['Wq'], 'L0_attn_Wk': _L0_attn_in['Wk'], 'L0_attn_Wv': _L0_attn_in['Wv'], 'L0_attn_Wo': _L0_attn_in['Wo'], 'L0_ffn_gate_weight': _L0_ffn_in['gate_weight'], 'L0_ffn_w1': _L0_ffn_in['w1'], 'L0_ffn_w2': _L0_ffn_in['w2'], 'L0_ffn_w3': _L0_ffn_in['w3'], 'L0_ffn_sw1': _L0_ffn_in['sw1'], 'L0_ffn_sw2': _L0_ffn_in['sw2'], 'L0_ffn_sw3': _L0_ffn_in['sw3']}
    _x0 = _d['L0_attn_x']
    _d['L0_attn_x'] = jax.random.normal(jax.random.fold_in(jax.random.key(seed), 1), (8, 512, 256), dtype=_x0.dtype)
    del _x0
    return _d

def reference(L0_attn_x, L0_attn_Wq, L0_attn_Wk, L0_attn_Wv, L0_attn_Wo, L0_ffn_gate_weight, L0_ffn_w1, L0_ffn_w2, L0_ffn_w3, L0_ffn_sw1, L0_ffn_sw2, L0_ffn_sw3):

    def _L0_attn_ref(x, Wq, Wk, Wv, Wo):
        import jax, jax.numpy as jnp
        import numpy as np
        EMBED_DIM = 256
        NUM_HEADS = 32
        HEAD_DIM = EMBED_DIM // NUM_HEADS
        BATCH = 2
        SEQ_LEN = 256
        q = jnp.einsum('bse,ef->bsf', x, Wq)
        k = jnp.einsum('bse,ef->bsf', x, Wk)
        v = jnp.einsum('bse,ef->bsf', x, Wv)
        qT = jnp.swapaxes(q, 1, 2)
        kT = jnp.swapaxes(k, 1, 2)
        vT = jnp.swapaxes(v, 1, 2)
        attn_scores = jnp.einsum('bes,bfs->bef', qT, kT) / np.sqrt(HEAD_DIM)
        attn_weights = jax.nn.softmax(attn_scores, axis=-1)
        attn_output = jnp.einsum('bef,bfs->bes', attn_weights, vT)
        attn_output = jnp.swapaxes(attn_output, 1, 2)
        return jnp.einsum('bse,ef->bsf', attn_output, Wo)

    def _L0_ffn_ref(hidden_states, gate_weight, w1, w2, w3, sw1, sw2, sw3):
        import jax, jax.numpy as jnp
        import numpy as np
        N_GROUP = 8
        TOPK_GROUP = 3
        TOP_K = 6
        ROUTED_SCALE = 1.0
        B, S, H = hidden_states.shape
        x = hidden_states.reshape(-1, H)
        T = x.shape[0]
        E = gate_weight.shape[0]
        logits = x.astype(jnp.float32) @ gate_weight.astype(jnp.float32).T
        scores = jax.nn.softmax(logits, axis=-1)
        per_group = E // N_GROUP
        group_scores = scores.reshape(T, N_GROUP, per_group).max(axis=-1)
        _, group_idx = jax.lax.top_k(group_scores, TOPK_GROUP)
        group_mask = jax.nn.one_hot(group_idx, N_GROUP, dtype=scores.dtype).sum(axis=1)
        score_mask = jnp.repeat(group_mask, per_group, axis=1)
        tmp_scores = jnp.where(score_mask > 0, scores, 0.0)
        topk_weight, topk_idx = jax.lax.top_k(tmp_scores, TOP_K)
        topk_weight = topk_weight / (topk_weight.sum(axis=-1, keepdims=True) + 1e-20)
        topk_weight = topk_weight * ROUTED_SCALE
        combine = jnp.zeros((T, E), scores.dtype).at[jnp.arange(T)[:, None], topk_idx].add(topk_weight)

        def body(acc, ws):
            ew1, ew2, ew3, ce = ws
            h = jax.nn.silu(x @ ew1.T) * (x @ ew3.T)
            return (acc + ce[:, None] * (h @ ew2.T), None)
        y, _ = jax.lax.scan(body, jnp.zeros_like(x), (w1, w2, w3, combine.T))
        shared = jax.nn.silu(x @ sw1.T) * (x @ sw3.T) @ sw2.T
        return (y + shared).reshape(B, S, H)
    x = L0_attn_x
    xn = _layernorm(x, axis=-1)
    s = _L0_attn_ref(xn, L0_attn_Wq, L0_attn_Wk, L0_attn_Wv, L0_attn_Wo)
    g = _silu(_L0_ffn_ref(xn, L0_ffn_gate_weight, L0_ffn_w1, L0_ffn_w2, L0_ffn_w3, L0_ffn_sw1, L0_ffn_sw2, L0_ffn_sw3))
    x = x + s * g
    return x

_drawn_inputs = setup_inputs


def setup_inputs(seed=0):
    import zlib

    import numpy as np

    out = dict(_drawn_inputs(seed))
    spreads = {}
    factors = {'L0_attn_Wq': 7.196,
     'L0_attn_Wk': 7.267,
     'L0_attn_Wv': 7.167,
     'L0_attn_Wo': 7.189,
     'L0_ffn_gate_weight': 8.0,
     'L0_ffn_w1': 8.0,
     'L0_ffn_w2': 8.0,
     'L0_ffn_w3': 8.0,
     'L0_ffn_sw1': 7.606,
     'L0_ffn_sw2': 7.551,
     'L0_ffn_sw3': 7.53}
    for name, (base, spread) in spreads.items():
        noise = np.random.default_rng([zlib.crc32(name.encode()), seed]).standard_normal(out[name].shape)
        drawn = base * np.exp(spread * noise) if base else spread * noise
        out[name] = jnp.asarray(drawn.astype(out[name].dtype))
    for name, factor in factors.items():
        out[name] = (out[name] * factor).astype(out[name].dtype)
    return out
```

```python
from contextlib import ExitStack

import numpy as np

import concourse.bass as bass
from concourse import mybir

ALU = mybir.AluOpType
ACT = mybir.ActivationFunctionType
F32 = mybir.dt.float32
BF16 = mybir.dt.bfloat16
I32 = mybir.dt.int32
AX_X = mybir.AxisListType.X

P = 128
B, S, H = 8, 512, 256
T = B * S
TILES = T // P
TB = S // P
HC = H // P
E, I, SI = 32, 128, 256
GROUPS, TOP_GROUPS, TOP_K = 8, 3, 6
PER_GROUP = E // GROUPS
HEAD_DIM = 8
SCALE = 1.0 / float(np.sqrt(HEAD_DIM))
EPS = 1e-5
SLOT_TILES = -(-T * TOP_K // P) + E
SURE_TILES = T * TOP_K // P
SLOTS = SLOT_TILES * P
EXTRA = 48
ROW = H + EXTRA
C_WEIGHT, C_TOKEN, C_SLOT = H, H + E, H + E + 1
NOWHERE = 1 << 20
WEXP = HC * 2 * I + H
RING = 4
SLOT_RING = 8
ACCS = 2


class Item:

    def __init__(self, base, c, unroll):
        self.base, self.c, self.unroll = base, c, unroll
        self.n = base + c
        self.static = isinstance(base, int)
        self.slot = c % unroll

    def rounds(self, each, back=0):
        return self.base * (each // self.unroll) + each * ((self.c - back) // self.unroll)

    def behind(self, k):
        return not self.static or self.n >= k


def settle(eng, waited, item):
    if not item.static:
        eng.sem_inc(waited, 1)


def rolled(eng, total, unroll, peel, body):
    for c in range(peel):
        body(Item(0, c, unroll))
    if peel < total:
        with eng.Fori(peel // unroll, total // unroll) as r:
            for c in range(unroll):
                body(Item(r * unroll, c, unroll))


def skewed(eng, total, stages, loop_from=2 * SLOT_RING, unroll=SLOT_RING):
    most = max(lead for _, lead in stages)
    least = min(lead for _, lead in stages)

    def step(base, c):
        for stage, lead in stages:
            if not isinstance(base, int) or 0 <= c + lead < total:
                stage(Item(base, c + lead, unroll))

    loop_to = (total - most) // unroll * unroll
    for s in range(-most, loop_from):
        step(0, s)
    with eng.Fori(loop_from // unroll, loop_to // unroll) as r:
        for c in range(unroll):
            step(r * unroll, c)
    for s in range(loop_to, total - least):
        step(0, s)


def gated_attention_moe(nc, x, wq, wk, wvT, wo, gwT, wexp, sw13T, sw2T, out):
    with ExitStack() as ctx:
        def sb(name, shape, dt=F32):
            return ctx.enter_context(nc.sbuf_tensor(name, shape, dt))

        def sem(name):
            return ctx.enter_context(nc.semaphore(name))

        def sems(name, n):
            return [sem(f"{name}{i}") for i in range(n)]

        rows_d = nc.dram_tensor("rows_d", [T, ROW], F32).ap()
        xnT_d = nc.dram_tensor("xnT_d", [B, P, HC * S], F32).ap()
        slots_d = nc.dram_tensor("slots_d", [SLOTS, ROW], F32).ap()
        acc_d = [nc.dram_tensor(f"acc{k}_d", [T, H], F32).ap() for k in range(ACCS)]
        rows_b = rows_d.rearrange("(b t p) c -> b p t c", t=TB, p=P)
        rows_t = rows_d.rearrange("(t p) c -> t p c", p=P)
        slots_t = slots_d.rearrange("(t p) c -> t p c", p=P)
        acc_b = [a.rearrange("(b t p) c -> b p t c", t=TB, p=P) for a in acc_d]
        x_b = x.rearrange("(b t p) c -> b p t c", t=TB, p=P)
        out_b = out.rearrange("(b t p) c -> b p t c", t=TB, p=P)

        w_all = sb("w_all", [P, E * WEXP])
        s_all = sb("s_all", [P, TILES * H])
        half = E * WEXP // 2
        full = TILES * E
        tmp = [w_all[:, half + k * full:half + (k + 1) * full] for k in range(12)]
        logits, expd, scores, masked, gt, eq, pref, sel, cnt_et, inc_et, pos, wts = tmp
        pair = w_all[0:1, half:half + SLOT_TILES * E]
        x_in = [s_all[:, k * TB * H:(k + 1) * TB * H].rearrange("p (t c) -> p t c", c=H) for k in range(2)]
        xn = [sb(f"xn{k}", [P, TB, H]) for k in range(2)]
        xnT = [sb(f"xnT{k}", [P, HC, S]) for k in range(2)]
        extra = sb("extra", [P, TILES, EXTRA])
        disp = sb("disp", [P, RING, ROW])
        pad = sb("pad", [P, ROW])
        w_q, w_k, w_vT, w_o = (sb(n, [P, HC, H]) for n in ("w_q", "w_k", "w_vT", "w_o"))
        g_w = sb("g_w", [P, HC, E])
        sw13 = sb("sw13", [P, 2, HC, SI])
        sw2 = sb("sw2", [P, HC, H])
        ident = sb("ident", [P, P])
        tri = sb("tri", [P, P], BF16)
        ones = sb("ones", [P, P], BF16)
        stats = sb("stats", [P, 2, TB, 6])
        mv = sb("mv", [P, 2, TB, 2])
        var, std, rough, rstd = (sb(n, [P, 2, TB]) for n in ("var", "std", "rough", "rstd"))
        newton = sb("newton", [P, TB])
        top8 = sb("top8", [P, TILES, 8])
        row1, row2, row3 = (sb(n, [P, TILES]) for n in ("row1", "row2", "row3"))
        totals, ends, begins, padded = (sb(n, [P, E]) for n in ("totals", "ends", "begins", "padded"))
        padded_i = sb("padded_i", [P, E], I32)
        last_i = sb("last_i", [1, E], I32)
        slot_tile_i = sb("slot_tile_i", [1, SLOT_TILES], I32)
        slot_tile = sb("slot_tile", [1, SLOT_TILES])
        expert_of = sb("expert_of", [1, SLOT_TILES])
        w_off = sb("w_off", [1, SLOT_TILES], I32)
        w_col = sb("w_col", [1, SLOT_TILES], I32)
        work = sb("work", [P, 9 * 512 + 2 * 1024])
        def part(at, n, **k):
            v = work[:, at:at + n]
            return v.rearrange("p (c n) -> p c n", **k) if k else v
        g_s, a_s, p_s, r_s, m_s = (part(512 * k, 512, c=HC) for k in range(5))
        silu_s = [part(2560 + 512 * k, 512) for k in range(2)]
        hT_s = part(3584, 1024, c=HC)
        y_s = [part(4608 + 1024 * k, 1024, c=TB) for k in range(2)]
        restart = part(0, full)
        sel16 = part(1024, full // 2).bitcast(BF16)
        restart8 = part(1536, TILES * GROUPS)
        gs, ggt, geq, gpref, gsel = (part(1792 + 256 * k, TILES * GROUPS) for k in range(5))
        mx, nmx, rsum, rinv = (sb(n, [P, HC]) for n in ("mx", "nmx", "rsum", "rinv"))
        slot = part(0, SLOT_RING * ROW, c=SLOT_RING)
        xT = [part(2432 + 256 * k, 256, c=HC) for k in range(2)]
        silu_e = [part(2944 + 128 * k, 128) for k in range(2)]
        h_e = [part(3200 + 128 * k, 128) for k in range(2)]
        hT_e = [part(3456 + 128 * k, 128) for k in range(2)]
        y_e = part(3712, SLOT_RING * H, c=SLOT_RING)
        def last(k):
            return w_all[:, k * TB * H:(k + 1) * TB * H].rearrange("p (t c) -> p t c", c=H)
        x_l, a_l, b_l, g_l, o_l = ([last(5 * k + n) for k in range(2)] for n in range(5))

        ps = ctx.enter_context(nc.psum_tensor("ps", [P, 8, 512], F32))

        s_waited_pool, s_waited_dve = sem("s_waited_pool"), sem("s_waited_dve")
        s_const = sem("s_const")
        s_w = sem("s_w")
        s_gw = sem("s_gw")
        s_wexp = sem("s_wexp")
        s_tail = sem("s_tail")
        s_x = sems("s_x", 2)
        s_stats = sem("s_stats")
        s_mv = sem("s_mv")
        s_var = sem("s_var")
        s_std = sem("s_std")
        s_rough = sem("s_rough")
        s_newton = sem("s_newton")
        s_rstd = sem("s_rstd")
        s_xn = sem("s_xn")
        s_xt_ps = sem("s_xt_ps")
        s_xt = sem("s_xt")
        s_lg_ps = sem("s_lg_ps")
        s_lg = sem("s_lg")
        s_stored = sems("s_stored", 2)
        s_chain = sem("s_chain")
        s_shift = sem("s_shift")
        s_exp = sem("s_exp")
        s_sel = sem("s_sel")
        s_cnt = sem("s_cnt")
        s_extra = sem("s_extra")
        s_last = sem("s_last")
        s_map = sem("s_map")
        s_extra_d = sem("s_extra_d")
        s_pads = sem("s_pads")
        s_ring = sems("s_ring", RING)
        s_disp = sems("s_disp", RING)
        s_l2 = sems("s_l2", 2)
        s_g_ps, s_a_ps, s_s_ps, s_r_ps, s_m_ps = (sem(f"s_{n}_ps") for n in "gasrm")
        s_g, s_a, s_p, s_r, s_m = (sem(f"s_{n}") for n in "gaprm")
        s_ab_ps = sem("s_ab_ps")
        s_silu = sem("s_silu")
        s_h = sem("s_h")
        s_y_ps = sem("s_y_ps")
        s_y = sem("s_y")
        s_at_ps = sem("s_at_ps")
        s_at = sem("s_at")
        s_mx = sem("s_mx")
        s_nmx = sem("s_nmx")
        s_ex = sem("s_ex")
        s_ri = sem("s_ri")
        s_acc0 = sems("s_acc0", 2)
        s_zero = sem("s_zero")
        s_slot = sems("s_slot", SLOT_RING)
        s_eT_ps, s_eab_ps, s_ehT_ps, s_ey_ps = (sem(n) for n in ("s_eT_ps", "s_eab_ps", "s_ehT_ps", "s_ey_ps"))
        s_eT, s_esilu, s_eh, s_ehT, s_ey = (sem(n) for n in ("s_eT", "s_esilu", "s_eh", "s_ehT", "s_ey"))
        s_add = sems("s_add", SLOT_RING)
        s_fin = sems("s_fin", 2)
        s_sum, s_gate, s_sg, s_o = (sem(n) for n in ("s_sum", "s_gate", "s_sg", "s_o"))
        s_out = sems("s_out", 2)

        block = ctx.enter_context(nc.Block())

        @block.sync
        def _(sp):
            def load_x(b):
                sp.dma_start(x_in[b.slot], x_b[b.n]).then_inc(s_x[b.slot], 16)

            def store_normed(b):
                sp.wait_ge(s_xn, b.n * TB + TB)
                sp.dma_start(rows_b[b.n, :, :, 0:H], xn[b.slot][:]).then_inc(s_stored[b.slot], 16)
                sp.wait_ge(s_xt, b.n * TB + TB)
                sp.dma_start(xnT_d[b.n], xnT[b.slot][:].rearrange("p c n -> p (c n)")).then_inc(s_stored[b.slot], 16)

            load_x(Item(0, 0, 2))
            load_x(Item(0, 1, 2))
            with sp.Fori(0, (B - 2) // 2) as r:
                for c in range(2):
                    sp.wait_ge(s_xn, r * (2 * TB) + (c + 1) * TB)
                    load_x(Item(r * 2, c + 2, 2))
                    store_normed(Item(r * 2, c, 2))
            for c in range(B - 2, B):
                store_normed(Item(0, c, 2))

            sp.wait_ge(s_last, 1)
            sp.wait_ge(s_tail, 16 * (SLOT_TILES - SURE_TILES))
            with sp.Fori(0, E) as e:
                r = sp.value_load(last_i[0:1, bass.ds(e, 1)], min_val=0, max_val=SLOTS - P)
                sp.dma_start(slots_d[bass.ds(r, P), :], pad[:]).then_inc(s_pads, 16)
            sp.wait_ge(s_extra, 1)
            sp.dma_start(rows_t[:, :, H:ROW].rearrange("t p c -> p t c"), extra[:]).then_inc(s_extra_d, 16)
            sp.wait_ge(s_extra_d, 16)
            for k in range(2):
                sp.wait_ge(s_stored[k], 32 * (B // 2))

            def load_rows(t):
                if t.behind(RING):
                    sp.wait_ge(s_disp[t.slot], t.rounds(16 * TOP_K))
                sp.dma_start(disp[:, t.slot, :], rows_t[t.n]).then_inc(s_ring[t.slot], 16)
            rolled(sp, TILES, RING, RING, load_rows)

            for k in range(RING):
                sp.wait_ge(s_disp[k], 16 * TOP_K * (TILES // RING))
            sp.wait_ge(s_at, 2 * B)
            sp.wait_ge(s_y, 2 * B)
            for k in range(2):
                sp.wait_ge(s_acc0[k], 16 * (B // 2))

            def load_slots(t):
                if t.behind(SLOT_RING):
                    sp.wait_ge(s_add[t.slot], t.rounds(16))
                sp.dma_start(slot[:, t.slot, :], slots_t[t.n]).then_inc(s_slot[t.slot], 16)
            rolled(sp, SLOT_TILES, SLOT_RING, SLOT_RING, load_slots)

            for k in range(SLOT_RING):
                sp.wait_ge(s_add[k], 16 * (SLOT_TILES // SLOT_RING))

            def load_last(b):
                for dst, src in ((x_l, x_b), (a_l, acc_b[0]), (b_l, acc_b[1])):
                    sp.dma_start(dst[b.slot], src[b.n]).then_inc(s_fin[b.slot], 16)

            def store_out(b):
                sp.wait_ge(s_o, b.n + 1)
                sp.dma_start(out_b[b.n], o_l[b.slot]).then_inc(s_out[b.slot], 16)
            load_last(Item(0, 0, 2))
            load_last(Item(0, 1, 2))
            with sp.Fori(0, (B - 2) // 2) as r:
                for c in range(2):
                    store_out(Item(r * 2, c, 2))
                    load_last(Item(r * 2, c + 2, 2))
            for c in range(B - 2, B):
                store_out(Item(0, c, 2))
            for k in range(2):
                sp.wait_ge(s_out[k], 16 * (B // 2))

        @block.gpsimd
        def _(pool):
            pool.memset(pad[:], 0.0).then_inc(s_const, 1)
            pool.memset(ident[:], 0.0).then_inc(s_const, 1)
            pool.memset(tri[:], 1.0).then_inc(s_const, 1)
            pool.memset(ones[:], 1.0).then_inc(s_const, 1)
            pool.memset(extra[:], 0.0).then_inc(s_const, 1)
            pool.memset(restart, 1.0).then_inc(s_const, 1)
            pool.memset(restart8, 1.0).then_inc(s_const, 1)
            pool.iota(slot_tile_i[:], pattern=[[1, SLOT_TILES]], base=0, channel_multiplier=0).then_inc(s_const, 1)
            pool.wait_ge(s_const, 8)
            pool.memset(pad[:, C_TOKEN:C_TOKEN + 1].bitcast(I32), NOWHERE).then_inc(s_const, 1)
            pool.affine_select(out=ident[:], in_=ident[:], compare_op=ALU.not_equal, fill=1.0,
                               base=0, pattern=[[-1, P]], channel_multiplier=1).then_inc(s_const, 1)
            pool.affine_select(out=tri[:], in_=tri[:], compare_op=ALU.is_gt, fill=0.0,
                               base=0, pattern=[[1, P]], channel_multiplier=-1).then_inc(s_const, 1)
            pool.iota(extra[:, :, C_TOKEN - H].bitcast(I32), pattern=[[P, TILES]], base=0,
                      channel_multiplier=1).then_inc(s_const, 1)
            pool.memset(restart.rearrange("p (t e) -> p t e", e=E)[:, :, 0:1], 0.0).then_inc(s_const, 1)
            pool.memset(restart8.rearrange("p (t g) -> p t g", g=GROUPS)[:, :, 0:1], 0.0).then_inc(s_const, 1)

            def inverse_std(b):
                v, r, t = var[:, b.slot, :], rough[:, b.slot, :], newton[:]
                pool.wait_ge(s_rough, b.n + 1)
                pool.tensor_tensor(t, r, r, ALU.mult).then_inc(s_newton, 1)
                pool.wait_ge(s_newton, b.n * 3 + 1)
                pool.tensor_tensor(t, t, v, ALU.mult).then_inc(s_newton, 1)
                pool.wait_ge(s_newton, b.n * 3 + 2)
                settle(pool, s_waited_pool, b)
                pool.tensor_scalar(t, t, -0.5, 1.5, ALU.mult, ALU.add).then_inc(s_newton, 1)
                pool.wait_ge(s_newton, b.n * 3 + 3)
                pool.tensor_tensor(rstd[:, b.slot, :], r, t, ALU.mult).then_inc(s_rstd, 1)
            rolled(pool, B, 2, 0, inverse_std)

            pool.wait_ge(s_pads, 16 * E)

            def scatter_rows(t):
                pool.wait_ge(s_ring[t.slot], t.rounds(16) + 16)
                settle(pool, s_waited_pool, t)
                for k in range(TOP_K):
                    at = disp[:, t.slot, C_SLOT + k:C_SLOT + k + 1].bitcast(I32)
                    pool.indirect_dma_start(slots_d[:, :], bass.IndirectOffsetOnAxis(ap=at, axis=0),
                                            disp[:, t.slot, :], None, bounds_check=SLOTS - 1,
                                            oob_is_err=False).then_inc(s_disp[t.slot], 16)
            rolled(pool, TILES, RING, 0, scatter_rows)

            def add_rows(t):
                pool.wait_ge(s_zero, 16 * TILES * (ACCS - 1))
                if t.behind(ACCS):
                    pool.wait_ge(s_add[(t.slot - ACCS) % SLOT_RING], t.rounds(16, back=ACCS) + 16)
                pool.wait_ge(s_ey, t.n + 1)
                settle(pool, s_waited_pool, t)
                to = slot[:, t.slot, C_TOKEN:C_TOKEN + 1].bitcast(I32)
                pool.indirect_dma_start(acc_d[t.slot % ACCS][:, :], bass.IndirectOffsetOnAxis(ap=to, axis=0),
                                        y_e[:, t.slot, :], None, bounds_check=T - 1, oob_is_err=False,
                                        compute_op=ALU.add).then_inc(s_add[t.slot], 16)
            rolled(pool, SLOT_TILES, SLOT_RING, SLOT_RING, add_rows)

            def gate(b):
                pool.wait_ge(s_gate, b.n + 1)
                pool.tensor_tensor(g_l[b.slot], g_l[b.slot],
                                   s_all[:, bass.ds(b.n * (TB * H), TB * H)].rearrange("p (t c) -> p t c", c=H),
                                   ALU.mult).then_inc(s_sg, 1)
            rolled(pool, B, 2, 0, gate)

        @block.scalar
        def _(act):
            for dst, src in ((w_q, wq), (w_k, wk), (w_vT, wvT), (w_o, wo), (sw2, sw2T)):
                act.dma_start(dst[:], src.rearrange("(c p) n -> p c n", p=P)).then_inc(s_w, 16)
            act.dma_start(sw13[:], sw13T.rearrange("w (c p) n -> p w c n", p=P)).then_inc(s_w, 16)
            act.dma_start(g_w[:], gwT.rearrange("(c p) n -> p c n", p=P)).then_inc(s_gw, 16)
            act.dma_start(w_all[:, 0:half], wexp[:, 0:half]).then_inc(s_wexp, 16)
            act.wait_ge(s_const, 14)
            with act.Fori(SURE_TILES, SLOT_TILES) as t:
                act.dma_start(slots_t[t], pad[:]).then_inc(s_tail, 16)

            for a in acc_b[1:]:
                with act.Fori(0, B) as b:
                    for t in range(TB):
                        act.dma_start(a[b, :, t, :], pad[:, 0:H]).then_inc(s_zero, 16)

            def root(b):
                act.wait_ge(s_var, b.n + 1)
                act.activation(std[:, b.slot, :], var[:, b.slot, :], ACT.Sqrt).then_inc(s_std, 1)

            def normed(b, more=True):
                if more:
                    root(Item(b.base, b.c + 1, 2))
                if b.behind(2):
                    act.wait_ge(s_stored[b.slot], b.rounds(32))
                for t in range(TB):
                    act.wait_ge(s_xt_ps, b.n * TB + t + 1)
                    act.activation(xnT[b.slot][:, :, t * P:(t + 1) * P],
                                   ps[:, t, 0:H].rearrange("p (c n) -> p c n", c=HC), ACT.Copy).then_inc(s_xt, 1)
                act.wait_ge(s_lg_ps, b.n + 1)
                act.activation(logits[:, bass.ds(b.n * (TB * E), TB * E)], ps[:, 4 + b.slot, 0:TB * E],
                               ACT.Copy).then_inc(s_lg, 1)
            root(Item(0, 0, 2))
            for c in range(2):
                normed(Item(0, c, 2))
            with act.Fori(1, (B - 2) // 2) as r:
                for c in range(2):
                    normed(Item(r * 2, c, 2))
            for c in range(B - 2, B):
                normed(Item(0, c, 2), more=c < B - 1)

            act.wait_ge(s_shift, 1)
            act.activation(expd, expd, ACT.Exp).then_inc(s_exp, 1)

            def load_batch(b):
                act.dma_start(xn[b.slot][:], rows_b[b.n, :, :, 0:H]).then_inc(s_l2[b.slot], 16)
                act.dma_start(xnT[b.slot][:].rearrange("p c n -> p (c n)"), xnT_d[b.n]).then_inc(s_l2[b.slot], 16)

            for k in range(2):
                act.wait_ge(s_stored[k], 32 * (B // 2))
            load_batch(Item(0, 0, 2))
            load_batch(Item(0, 1, 2))

            def batch(b, more=True):
                act.wait_ge(s_g_ps, b.n + 1)
                act.activation(g_s, ps[:, 0, :].rearrange("p (c n) -> p c n", c=HC), ACT.Copy).then_inc(s_g, 1)
                for m in range(HC):
                    act.wait_ge(s_ab_ps, b.n * HC + m + 1)
                    act.activation(silu_s[m], ps[:, 4 + 2 * m, :], ACT.Silu).then_inc(s_silu, 1)
                for n in range(2):
                    if n == 0 and b.behind(2):
                        act.wait_ge(s_acc0[b.slot], b.rounds(16))
                    act.wait_ge(s_y_ps, b.n * 2 + n + 1)
                    act.activation(y_s[b.slot][:, 2 * n:2 * n + 2, :],
                                   ps[:, 4 + n, :].rearrange("p (t c) -> p t c", c=H), ACT.Copy).then_inc(s_y, 1)
                act.wait_ge(s_nmx, b.n + 1)
                for c in range(HC):
                    act.activation(p_s[:, c, :], ps[:, 0, c * H:(c + 1) * H], ACT.Exp, bias=nmx[:, c:c + 1],
                                   scale=SCALE, accum_out=rsum[:, c:c + 1]).then_inc(s_ex, 1)
                act.wait_ge(s_y, b.n * 2 + 2)
                act.dma_start(acc_b[0][b.n], y_s[b.slot]).then_inc(s_acc0[b.slot], 16)
                act.wait_ge(s_r_ps, b.n + 1)
                act.activation(r_s, ps[:, 1, :].rearrange("p (c n) -> p c n", c=HC), ACT.Copy).then_inc(s_r, 1)
                if more:
                    act.wait_ge(s_at_ps, b.n * 2 + 2)
                    load_batch(Item(b.base, b.c + 2, 2))
            batch(Item(0, 0, 2))
            act.wait_ge(s_map, 1)
            act.dma_start(w_all[:, half:], wexp[:, half:]).then_inc(s_wexp, 16)
            batch(Item(0, 1, 2))
            with act.Fori(1, (B - 2) // 2) as r:
                for c in range(2):
                    batch(Item(r * 2, c, 2))
            for c in range(B - 2, B):
                batch(Item(0, c, 2), more=False)

            act.wait_ge(s_map, 1)
            act.wait_ge(s_at, 2 * B)

            def silu(t):
                if t.behind(2):
                    act.wait_ge(s_eh, t.n - 1)
                act.wait_ge(s_eab_ps, t.n + 1)
                act.activation(silu_e[t.slot % 2], ps[:, 2 + t.slot % 2, 0:I], ACT.Silu).then_inc(s_esilu, 1)

            def turned_hidden(t):
                act.wait_ge(s_ehT_ps, t.n + 1)
                act.activation(hT_e[t.slot % 2], ps[:, 4 + t.slot % 2, 0:P], ACT.Copy).then_inc(s_ehT, 1)

            def weigh(t):
                col = act.value_load(w_col[0:1, bass.ds(t.n, 1)], min_val=C_WEIGHT, max_val=C_WEIGHT + E - 1)
                if t.behind(SLOT_RING):
                    act.wait_ge(s_add[t.slot], t.rounds(16))
                act.wait_ge(s_ey_ps, t.n + 1)
                act.activation(y_e[:, t.slot, :], ps[:, 6 + t.slot % 2, 0:H], ACT.Copy,
                               scale=slot[:, t.slot, bass.ds(col, 1)]).then_inc(s_ey, 1)
            skewed(act, SLOT_TILES, [(silu, 1), (turned_hidden, 0), (weigh, -1)])

            def gate(b):
                act.wait_ge(s_sum, b.n + 1)
                if b.behind(2):
                    act.wait_ge(s_o, b.n - 1)
                act.activation(g_l[b.slot], a_l[b.slot], ACT.Silu).then_inc(s_gate, 1)
            rolled(act, B, 2, 2, gate)

        @block.tensor
        def _(pe):
            pe.wait_ge(s_const, 14)
            pe.wait_ge(s_gw, 16)

            def normed(b):
                for t in range(TB):
                    pe.wait_ge(s_xn, b.n * TB + t + 1)
                    if b.behind(1):
                        pe.wait_ge(s_xt, b.n * TB + (t + 1 - TB))
                    for c in range(HC):
                        mm = pe.transpose(ps[:, t, c * P:(c + 1) * P], xn[b.slot][:, t, c * P:(c + 1) * P], ident[:])
                    mm.then_inc(s_xt_ps, 1)
                if b.behind(2):
                    pe.wait_ge(s_lg, b.n - 1)
                for t in range(TB):
                    pe.wait_ge(s_xt, b.n * TB + t + 1)
                    for c in range(HC):
                        mm = pe.matmul(ps[:, 4 + b.slot, t * E:(t + 1) * E], xnT[b.slot][:, c, t * P:(t + 1) * P],
                                       g_w[:, c, :], start=(c == 0), stop=(c == HC - 1))
                mm.then_inc(s_lg_ps, 1)
            rolled(pe, B, 2, 2, normed)

            pe.wait_ge(s_sel, 1)
            pe.wait_ge(s_xt, TILES)
            for k in range(2):
                pe.matmul(ps[:, 2 + k, :], ones[:], sel16[:, k * 512:(k + 1) * 512], start=True, stop=True).then_inc(s_cnt, 1)
            for k in range(2):
                pe.matmul(ps[:, k, :], tri[:], sel16[:, k * 512:(k + 1) * 512], start=True, stop=True).then_inc(s_cnt, 1)

            pe.wait_ge(s_w, 16 * 6)
            pe.wait_ge(s_extra, 1)

            def product(bank, lhs, rhs, done):
                for m in range(HC):
                    for k in range(HC):
                        mm = pe.matmul(ps[:, bank, m * H:(m + 1) * H], lhs[:, k, m * P:(m + 1) * P], rhs[:, k, :],
                                       start=(k == 0), stop=(k == HC - 1))
                mm.then_inc(done, 1)

            def batch(b):
                xb, xt = xn[b.slot], xnT[b.slot]
                pe.wait_ge(s_l2[b.slot], b.rounds(32) + 32)
                if b.behind(1):
                    pe.wait_ge(s_m, b.n)
                for m in range(HC):
                    for t in range(TB):
                        mm = pe.matmul(ps[:, 0, m * H:(m + 1) * H], xb[:, t, m * P:(m + 1) * P], xb[:, t, :],
                                       start=(t == 0), stop=(t == TB - 1))
                mm.then_inc(s_g_ps, 1)
                if b.behind(1):
                    pe.wait_ge(s_y, b.n * 2)
                    pe.wait_ge(s_h, b.n * HC)
                for m in range(HC):
                    for w in range(2):
                        for k in range(HC):
                            mm = pe.matmul(ps[:, 4 + 2 * m + w, :], sw13[:, w, k, m * P:(m + 1) * P], xt[:, k, :],
                                           start=(k == 0), stop=(k == HC - 1))
                    mm.then_inc(s_ab_ps, 1)
                    if m == 0:
                        pe.wait_ge(s_g, b.n + 1)
                        if b.behind(1):
                            pe.wait_ge(s_r, b.n)
                        product(1, g_s, w_k, s_a_ps)
                pe.wait_ge(s_a, b.n + 1)
                product(0, w_q, a_s, s_s_ps)
                for n in range(2):
                    pe.wait_ge(s_h, b.n * HC + HC)
                    for t in range(2):
                        for k in range(HC):
                            at = (2 * n + t) * P
                            mm = pe.matmul(ps[:, 4 + n, t * H:(t + 1) * H], hT_s[:, k, at:at + P], sw2[:, k, :],
                                           start=(k == 0), stop=(k == HC - 1))
                    mm.then_inc(s_y_ps, 1)
                pe.wait_ge(s_p, b.n * HC + HC)
                product(1, p_s, w_o, s_r_ps)
                pe.wait_ge(s_r, b.n + 1)
                product(0, w_vT, r_s, s_m_ps)
                pe.wait_ge(s_m, b.n + 1)
                if b.behind(1):
                    pe.wait_ge(s_at, b.n * 2)
                for n in range(2):
                    for t in range(2):
                        for k in range(HC):
                            at = (2 * n + t) * P
                            mm = pe.matmul(ps[:, 2 + n, t * H:(t + 1) * H], xt[:, k, at:at + P], m_s[:, k, :],
                                           start=(k == 0), stop=(k == HC - 1))
                    mm.then_inc(s_at_ps, 1)
            rolled(pe, B, 2, 2, batch)

            pe.wait_ge(s_map, 1)
            pe.wait_ge(s_wexp, 32)
            pe.wait_ge(s_at, 2 * B)

            def turn_rows(t):
                pe.wait_ge(s_slot[t.slot], t.rounds(16) + 16)
                if t.behind(2):
                    pe.wait_ge(s_eT, t.n - 1)
                for c in range(HC):
                    mm = pe.transpose(ps[:, t.slot % 2, c * P:(c + 1) * P], slot[:, t.slot, c * P:(c + 1) * P], ident[:])
                mm.then_inc(s_eT_ps, 1)

            def hidden(t):
                off = pe.value_load(w_off[0:1, bass.ds(t.n, 1)], min_val=0, max_val=(E - 1) * WEXP)
                pe.wait_ge(s_eT, t.n + 1)
                if t.behind(2):
                    pe.wait_ge(s_eh, t.n - 1)
                for k in range(HC):
                    mm = pe.matmul(ps[:, 2 + t.slot % 2, 0:2 * I], xT[t.slot % 2][:, k, :],
                                   w_all[:, bass.ds(off + k * 2 * I, 2 * I)], start=(k == 0), stop=(k == HC - 1))
                mm.then_inc(s_eab_ps, 1)

            def turn_hidden(t):
                pe.wait_ge(s_eh, t.n + 1)
                if t.behind(2):
                    pe.wait_ge(s_ehT, t.n - 1)
                pe.transpose(ps[:, 4 + t.slot % 2, 0:P], h_e[t.slot % 2], ident[:]).then_inc(s_ehT_ps, 1)

            def expert_out(t):
                off = pe.value_load(w_off[0:1, bass.ds(t.n, 1)], min_val=0, max_val=(E - 1) * WEXP)
                pe.wait_ge(s_ehT, t.n + 1)
                if t.behind(2):
                    pe.wait_ge(s_ey, t.n - 1)
                pe.matmul(ps[:, 6 + t.slot % 2, 0:H], hT_e[t.slot % 2], w_all[:, bass.ds(off + HC * 2 * I, H)],
                          start=True, stop=True).then_inc(s_ey_ps, 1)
            skewed(pe, SLOT_TILES, [(turn_rows, 2), (hidden, 1), (turn_hidden, 0), (expert_out, -1)])

        @block.vector
        def _(dve):
            links = [0]

            def then(ins):
                links[0] += 1
                ins.then_inc(s_chain, 1)
                dve.wait_ge(s_chain, links[0])

            def moments(b):
                dve.wait_ge(s_x[b.slot], b.rounds(16) + 16)
                for t in range(TB):
                    dve.bn_stats(stats[:, b.slot, t, :], x_in[b.slot][:, t, :]).then_inc(s_stats, 1)
                dve.wait_ge(s_stats, b.n * TB + TB)
                settle(dve, s_waited_dve, b)
                for t in range(TB):
                    dve.bn_aggr(mv[:, b.slot, t, :], stats[:, b.slot, t, :]).then_inc(s_mv, 1)
                dve.wait_ge(s_mv, b.n * TB + TB)
                if b.behind(2):
                    dve.wait_ge(s_rstd, b.n - 1)
                dve.tensor_scalar(var[:, b.slot, :], mv[:, b.slot, :, 1], EPS, None, ALU.add).then_inc(s_var, 1)

            def invert(b):
                dve.wait_ge(s_std, b.n + 1)
                dve.reciprocal(rough[:, b.slot, :], std[:, b.slot, :]).then_inc(s_rough, 1)

            def normed(b):
                dve.wait_ge(s_rstd, b.n + 1)
                if b.behind(2):
                    dve.wait_ge(s_stored[b.slot], b.rounds(32))
                for t in range(TB):
                    dve.tensor_scalar(xn[b.slot][:, t, :], x_in[b.slot][:, t, :], mv[:, b.slot, t, 0:1],
                                      rstd[:, b.slot, t:t + 1], ALU.subtract, ALU.mult).then_inc(s_xn, 1)

            def step(base, c):
                moments(Item(base, c + 1, 2))
                normed(Item(base, c, 2))
                invert(Item(base, c + 1, 2))
            moments(Item(0, 0, 2))
            invert(Item(0, 0, 2))
            for c in range(2):
                step(0, c)
            with dve.Fori(1, (B - 2) // 2) as r:
                for c in range(2):
                    step(r * 2, c)
            step(0, B - 2)
            normed(Item(0, B - 1, 2))

            def by(v, n):
                return v.rearrange("p (t e) -> p t e", e=n)

            def spread(v, n):
                return v.unsqueeze(2).to_broadcast([P, v.shape[1], n])

            def choose(vals, n, k, above, same, prefix, chosen, again):
                for t in range(TILES):
                    ins = dve.max(top8[:, t, :], vals[:, t * n:(t + 1) * n])
                then(ins)
                kth = top8[:, :, k - 1:k].to_broadcast([P, TILES, n])
                dve.tensor_tensor(by(above, n), by(vals, n), kth, ALU.is_gt)
                then(dve.tensor_tensor(by(same, n), by(vals, n), kth, ALU.is_equal))
                dve.tensor_reduce(row1[:], by(above, n), AX_X, ALU.add)
                then(dve.tensor_tensor_scan(prefix, again, same, 0.0, ALU.mult, ALU.add))
                then(dve.tensor_scalar(row2[:], row1[:], -1.0, float(k), ALU.mult, ALU.add))
                then(dve.tensor_tensor(by(prefix, n), by(prefix, n), spread(row2[:], n), ALU.is_le))
                then(dve.tensor_tensor(same, same, prefix, ALU.mult))
                then(dve.tensor_tensor(chosen, above, same, ALU.add))

            dve.wait_ge(s_const, 14)
            dve.wait_ge(s_lg, B)
            then(dve.tensor_reduce(row1[:], by(logits, E), AX_X, ALU.max))
            dve.tensor_tensor(by(expd, E), by(logits, E), spread(row1[:], E), ALU.subtract).then_inc(s_shift, 1)
            dve.wait_ge(s_exp, 1)
            then(dve.tensor_reduce(row2[:], by(expd, E), AX_X, ALU.add))
            then(dve.reciprocal(row3[:], row2[:]))
            then(dve.tensor_tensor(by(scores, E), by(expd, E), spread(row3[:], E), ALU.mult))
            then(dve.tensor_reduce(gs, scores.rearrange("p (n g) -> p n g", g=PER_GROUP), AX_X, ALU.max))
            choose(gs, GROUPS, TOP_GROUPS, ggt, geq, gpref, gsel, restart8)
            then(dve.tensor_tensor(masked.rearrange("p (n g) -> p n g", g=PER_GROUP),
                                   scores.rearrange("p (n g) -> p n g", g=PER_GROUP),
                                   gsel.unsqueeze(2).to_broadcast([P, TILES * GROUPS, PER_GROUP]), ALU.mult))
            choose(masked, E, TOP_K, gt, eq, pref, sel, restart)
            dve.tensor_copy(sel16, sel).then_inc(s_sel, 1)
            dve.wait_ge(s_cnt, 4)
            then(dve.tensor_copy(cnt_et.rearrange("p (e t) -> p t e", t=TILES), ps[:, 2:4, :].rearrange("p b (t e) -> p (b t) e", e=E)))
            then(dve.tensor_tensor_scan(inc_et, restart, cnt_et, 0.0, ALU.mult, ALU.add))
            dve.tensor_tensor(cnt_et, inc_et, cnt_et, ALU.subtract)
            then(dve.tensor_scalar(padded_i[:], inc_et.rearrange("p (e t) -> p e t", t=TILES)[:, :, TILES - 1], float(P - 1), None, ALU.add))
            then(dve.tensor_scalar(padded_i[:], padded_i[:], -P, None, ALU.bitwise_and))
            then(dve.tensor_copy(padded[:], padded_i[:]))
            then(dve.tensor_tensor_scan(ends[:], padded[:], padded[:], 0.0, ALU.add, ALU.bypass))
            then(dve.tensor_tensor(begins[:], ends[:], padded[:], ALU.subtract))
            dve.tensor_scalar(last_i[:], ends[0:1, :], float(-P), 0.0, ALU.add, ALU.max).then_inc(s_last, 1)
            then(dve.tensor_tensor(cnt_et.rearrange("p (e t) -> p e t", t=TILES), cnt_et.rearrange("p (e t) -> p e t", t=TILES),
                                   spread(begins[:], TILES), ALU.add))
            then(dve.tensor_tensor(by(pos, E), ps[:, 0:2, :].rearrange("p b (t e) -> p (b t) e", e=E),
                                   cnt_et.rearrange("p (e t) -> p t e", t=TILES), ALU.add))
            then(dve.scalar_tensor_tensor(pos, pos, 1.0, sel, ALU.add, ALU.mult))
            for t in range(TILES):
                ins = dve.max(top8[:, t, :], pos[:, t * E:(t + 1) * E])
            then(ins)
            dve.tensor_scalar(extra[:, :, C_SLOT - H:C_SLOT - H + TOP_K].bitcast(I32), top8[:, :, 0:TOP_K], -1.0, None, ALU.add)
            then(dve.tensor_tensor(wts, masked, sel, ALU.mult))
            then(dve.tensor_reduce(row1[:], by(wts, E), AX_X, ALU.add))
            then(dve.tensor_scalar(row2[:], row1[:], 1e-20, None, ALU.add))
            then(dve.reciprocal(row3[:], row2[:]))
            dve.tensor_tensor(extra[:, :, 0:E], by(wts, E), spread(row3[:], E), ALU.mult).then_inc(s_extra, 1)
            then(dve.tensor_copy(slot_tile[:], slot_tile_i[:]))
            then(dve.tensor_scalar(totals[:], ends[:], 1.0 / P, None, ALU.mult))
            pairs = pair.rearrange("p (t e) -> p t e", e=E)
            then(dve.tensor_tensor(pairs, totals[0:1, :].unsqueeze(1).to_broadcast([1, SLOT_TILES, E]),
                                   slot_tile[:].unsqueeze(2).to_broadcast([1, SLOT_TILES, E]), ALU.is_le))
            then(dve.tensor_reduce(expert_of[:], pairs, AX_X, ALU.add))
            then(dve.tensor_scalar(expert_of[:], expert_of[:], float(E - 1), None, ALU.min))
            then(dve.tensor_scalar(w_off[:], expert_of[:], float(WEXP), None, ALU.mult))
            dve.tensor_scalar(w_col[:], expert_of[:], float(C_WEIGHT), None, ALU.add).then_inc(s_map, 1)

            def hidden(b, m):
                dve.wait_ge(s_silu, b.n * HC + m + 1)
                dve.tensor_tensor(hT_s[:, m, :], silu_s[m], ps[:, 5 + 2 * m, :], ALU.mult).then_inc(s_h, 1)

            def batch(b):
                hidden(b, 0)
                dve.wait_ge(s_a_ps, b.n + 1)
                dve.tensor_copy(a_s, ps[:, 1, :].rearrange("p (c n) -> p c n", c=HC)).then_inc(s_a, 1)
                hidden(b, 1)
                dve.wait_ge(s_s_ps, b.n + 1)
                dve.tensor_reduce(mx[:], ps[:, 0, :].rearrange("p (c n) -> p c n", c=HC), AX_X, ALU.max).then_inc(s_mx, 1)
                dve.wait_ge(s_mx, b.n + 1)
                dve.tensor_scalar(nmx[:], mx[:], -SCALE, None, ALU.mult).then_inc(s_nmx, 1)
                dve.wait_ge(s_ex, b.n * HC + HC)
                dve.reciprocal(rinv[:], rsum[:]).then_inc(s_ri, 1)
                dve.wait_ge(s_ri, b.n + 1)
                for c in range(HC):
                    dve.tensor_scalar(p_s[:, c, :], p_s[:, c, :], rinv[:, c:c + 1], None, ALU.mult).then_inc(s_p, 1)
                dve.wait_ge(s_m_ps, b.n + 1)
                dve.tensor_copy(m_s, ps[:, 0, :].rearrange("p (c n) -> p c n", c=HC)).then_inc(s_m, 1)
                for n in range(2):
                    dve.wait_ge(s_at_ps, b.n * 2 + n + 1)
                    dve.tensor_copy(s_all[:, bass.ds(b.n * (TB * H) + n * 2 * H, 2 * H)], ps[:, 2 + n, :]).then_inc(s_at, 1)
            rolled(dve, B, 2, 0, batch)

            def turned_rows(t):
                dve.wait_ge(s_eT_ps, t.n + 1)
                if t.behind(2):
                    dve.wait_ge(s_eab_ps, t.n - 1)
                dve.tensor_copy(xT[t.slot % 2], ps[:, t.slot % 2, 0:H].rearrange("p (c n) -> p c n", c=HC)).then_inc(s_eT, 1)

            def hidden_rows(t):
                dve.wait_ge(s_esilu, t.n + 1)
                if t.behind(2):
                    dve.wait_ge(s_ehT_ps, t.n - 1)
                dve.tensor_tensor(h_e[t.slot % 2], silu_e[t.slot % 2], ps[:, 2 + t.slot % 2, I:2 * I], ALU.mult).then_inc(s_eh, 1)
            skewed(dve, SLOT_TILES, [(turned_rows, 2), (hidden_rows, 1)])

            def sum_y(b):
                dve.wait_ge(s_fin[b.slot], b.rounds(16 * (1 + ACCS)) + 16 * (1 + ACCS))
                dve.tensor_tensor(a_l[b.slot], a_l[b.slot], b_l[b.slot], ALU.add).then_inc(s_sum, 1)

            def finish(b):
                dve.wait_ge(s_sg, b.n + 1)
                if b.behind(2):
                    dve.wait_ge(s_out[b.slot], b.rounds(16))
                dve.tensor_tensor(o_l[b.slot], g_l[b.slot], x_l[b.slot], ALU.add).then_inc(s_o, 1)
            sum_y(Item(0, 0, 2))
            for c in range(2):
                sum_y(Item(0, c + 1, 2))
                finish(Item(0, c, 2))
            with dve.Fori(1, (B - 2) // 2) as r:
                for c in range(2):
                    sum_y(Item(r * 2, c + 1, 2))
                    finish(Item(r * 2, c, 2))
            sum_y(Item(0, B - 1, 2))
            finish(Item(0, B - 2, 2))
            finish(Item(0, B - 1, 2))


def kernel(L0_attn_x, L0_attn_Wq, L0_attn_Wk, L0_attn_Wv, L0_attn_Wo, L0_ffn_gate_weight, L0_ffn_w1, L0_ffn_w2,
           L0_ffn_w3, L0_ffn_sw1, L0_ffn_sw2, L0_ffn_sw3):
    import concourse.bacc as bacc
    from concourse.bass_utils import run_bass_kernel_spmd as run

    def lay(a):
        return np.ascontiguousarray(a)

    a = {
        "x": lay(np.asarray(L0_attn_x).reshape(T, H)),
        "wq": lay(np.asarray(L0_attn_Wq)),
        "wk": lay(np.asarray(L0_attn_Wk)),
        "wvT": lay(np.asarray(L0_attn_Wv).T),
        "wo": lay(np.asarray(L0_attn_Wo)),
        "gwT": lay(np.asarray(L0_ffn_gate_weight).T),
    }
    w13 = np.stack([np.asarray(L0_ffn_w1), np.asarray(L0_ffn_w3)])
    w13 = w13.reshape(2, E, I, HC, P).transpose(4, 1, 3, 0, 2).reshape(P, E, HC * 2 * I)
    w2 = np.asarray(L0_ffn_w2).transpose(2, 0, 1)
    a["wexp"] = lay(np.concatenate([w13, w2], axis=2).reshape(P, E * WEXP))
    a["sw13T"] = lay(np.stack([np.asarray(L0_ffn_sw1).T, np.asarray(L0_ffn_sw3).T]))
    a["sw2T"] = lay(np.asarray(L0_ffn_sw2).T)

    nc = bacc.Bacc("TRN2", target_bir_lowering=False, num_devices=1)
    aps = [nc.dram_tensor(f"in_{n}", v.shape, mybir.dt.from_np(v.dtype), kind="ExternalInput").ap() for n, v in a.items()]
    out = nc.dram_tensor("out", (T, H), F32, kind="ExternalOutput").ap()
    gated_attention_moe(nc, *aps, out)
    r = run(nc, [{f"in_{n}": v for n, v in a.items()}], core_ids=[0])
    return r.results[0]["out"].reshape(B, S, H)
```

```python
from contextlib import ExitStack

import numpy as np

import concourse.bass as bass
from concourse import mybir

ALU = mybir.AluOpType
ACT = mybir.ActivationFunctionType
F32 = mybir.dt.float32
BF16 = mybir.dt.bfloat16
I32 = mybir.dt.int32
AX_X = mybir.AxisListType.X

P = 128
B, S, H = 8, 512, 256
T = B * S
TILES = T // P
TB = S // P
HC = H // P
E, I, SI = 32, 128, 256
GROUPS, TOP_GROUPS, TOP_K = 8, 3, 6
PER_GROUP = E // GROUPS
HEAD_DIM = 8
SCALE = 1.0 / float(np.sqrt(HEAD_DIM))
EPS = 1e-5
SLOT_TILES = T * TOP_K // P + E
REGION = P + T
SLOTS = E * REGION + P
EXTRA = 48
ROW = H + EXTRA
C_WEIGHT, C_TOKEN, C_SLOT = H, H + E, H + E + 1
LAST_RING = 4
WEXP = HC * 2 * I + H
W_STEP = (E - 4) * WEXP // B
SLOT_RING = 8
ACCS = 2


class Item:

    def __init__(self, base, c, unroll):
        self.base, self.c, self.unroll = base, c, unroll
        self.n = base + c
        self.static = isinstance(base, int)
        self.slot = c % unroll

    def rounds(self, each, back=0):
        return self.base * (each // self.unroll) + each * ((self.c - back) // self.unroll)

    def behind(self, k):
        return not self.static or self.n >= k


def settle(eng, waited, item):
    if not item.static:
        eng.sem_inc(waited, 1)


def rolled(eng, total, unroll, peel, body):
    for c in range(peel):
        body(Item(0, c, unroll))
    if peel < total:
        with eng.Fori(peel // unroll, total // unroll) as r:
            for c in range(unroll):
                body(Item(r * unroll, c, unroll))


def registers(nc, engine, table, at, n, most):
    return nc.values_load_multi_w_load_instructions(
        table[0:1, bass.ds(at + 1, n)], engines=[engine], min_val=0, max_val=most,
        skip_runtime_bounds_check_because="the tables' entries are bounded where they are computed")[1]


def skewed(eng, total, stages, numbers=None, loop_from=2 * SLOT_RING, unroll=SLOT_RING):
    most = max(lead for _, lead in stages)
    least = min(lead for _, lead in stages)

    def step(base, c, loaded=None):
        for stage, lead in stages:
            if isinstance(base, int) and not 0 <= c + lead < total:
                continue
            item = Item(base, c + lead, unroll)
            if numbers:
                item.number = loaded[c + lead - least] if loaded else lambda n=item.n: numbers(n, 1)[0]
            stage(item)

    loop_to = (total - most) // unroll * unroll
    for s in range(-most, loop_from):
        step(0, s)
    with eng.Fori(loop_from // unroll, loop_to // unroll) as r:
        loaded = [lambda v=v: v for v in numbers(r * unroll + least, unroll + most - least)] if numbers else None
        for c in range(unroll):
            step(r * unroll, c, loaded)
    for s in range(loop_to, total - least):
        step(0, s)


def gated_attention_moe(nc, x, wq, wk, wvT, wo, gwT, wexp, sw13T, sw2T, out):
    with ExitStack() as ctx:
        def sb(name, shape, dt=F32):
            return ctx.enter_context(nc.sbuf_tensor(name, shape, dt))

        def sem(name):
            return ctx.enter_context(nc.semaphore(name))

        def sems(name, n):
            return [sem(f"{name}{i}") for i in range(n)]

        slots_d = nc.dram_tensor("slots_d", [SLOTS, ROW], F32).ap()
        table_d = nc.dram_tensor("table_d", [3, 2 * P], I32).ap()
        acc_d = [nc.dram_tensor(f"acc{k}_d", [T + P, H], F32).ap() for k in range(ACCS)]
        acc_b = [a[0:T].rearrange("(b t p) c -> b p t c", t=TB, p=P) for a in acc_d]
        x_b = x.rearrange("(b t p) c -> b p t c", t=TB, p=P)
        out_b = out.rearrange("(b t p) c -> b p t c", t=TB, p=P)

        w_all = sb("w_all", [P, E * WEXP])
        s_all = sb("s_all", [P, TILES * H])
        places = {"at": 0}
        early = sb("early", [P, 10000])

        def carve(n, dt=F32):
            places["at"] += n
            v = early[:, places["at"] - n:places["at"]]
            return v if dt == F32 else v.bitcast(dt)

        def chunks(v, c=HC):
            return v.rearrange("p (c n) -> p c n", c=c)

        disp = [carve(TB * ROW).rearrange("p (t c) -> p t c", c=ROW) for _ in range(2)]
        xn = [chunks(carve(TB * H), TB) for _ in range(2)]
        xnT = [chunks(carve(HC * S)) for _ in range(2)]
        w_q, w_k, w_vT, w_o, sw2 = (chunks(carve(HC * H)) for _ in range(5))
        x_last = early[:, 0:TILES * H]
        sw13 = sb("sw13", [P, 2, HC, SI])
        g_w = sb("g_w", [P, HC, E])
        pad = sb("pad", [P, ROW])
        ident = sb("ident", [P, P])
        tri = sb("tri", [P, P], BF16)
        ones = sb("ones", [P, P], BF16)
        work = sb("work", [P, 9 * 512 + 2 * 1024])

        def part(at, n, c=None):
            return chunks(work[:, at:at + n], c) if c else work[:, at:at + n]
        g_s, a_s, p_s, r_s, m_s = (part(512 * k, 512, HC) for k in range(5))
        silu_s = [part(2560 + 512 * k, 512) for k in range(2)]
        hT_s = part(3584, 1024, HC)
        y_s = [part(4608 + 1024 * k, 1024, TB) for k in range(2)]
        mx, nmx, rsum, rinv = (sb(n, [P, HC]) for n in ("mx", "nmx", "rsum", "rinv"))
        slot = part(0, SLOT_RING * ROW, SLOT_RING)
        xT = [part(2432 + 256 * k, 256, HC) for k in range(2)]
        silu_e = [part(2944 + 128 * k, 128) for k in range(2)]
        h_e = [part(3200 + 128 * k, 128) for k in range(2)]
        hT_e = [part(3456 + 128 * k, 128) for k in range(2)]
        y_e = part(3712, SLOT_RING * H, SLOT_RING)
        full, gfull = TB * E, TB * GROUPS
        w_early = (E - 4) * WEXP
        tmp = [w_all[:, w_early + k * full:w_early + (k + 1) * full] for k in range(13)]
        logits, shifted, expd, scores, masked, gt, eq, pref, sel, cnt_et, inc_et, pos, wts = tmp
        gtmp = [w_all[:, w_early + 13 * full + k * gfull:w_early + 13 * full + (k + 1) * gfull] for k in range(5)]
        gs, ggt, geq, gpref, gsel = gtmp
        sel16 = sb("sel16", [P, full], BF16)
        restart = sb("restart", [P, full])
        restart4 = sb("restart4", [P, full])
        restart8 = sb("restart8", [P, gfull])
        top8 = sb("top8", [P, TB, 8])
        row1, row2, row3 = (sb(n, [P, TB]) for n in ("row1", "row2", "row3"))
        token = sb("token", [P, TB])
        token_i = sb("token_i", [P, TB], I32)
        first_i, used = sb("first_i", [P, E], I32), sb("used", [P, E])
        first = sb("first", [P, E])
        ends, padded, shift, jump = (sb(n, [P, E]) for n in ("ends", "padded", "shift", "jump"))
        padded_i = sb("padded_i", [P, E], I32)
        tile_i = sb("tile_i", [P, 2], I32)
        tile_f = sb("tile_f", [P, 2])
        pairs, jumps = sb("pairs", [P, 2, E]), sb("jumps", [P, 2, E])
        expert, begin = sb("expert", [P, 2]), sb("begin", [P, 2])
        table = sb("table", [P, 3, 2], I32)
        tables = [sb(n, [1, 8 + 2 * P], I32) for n in ("w_off", "w_col", "w_row")]
        w_off, w_col, w_row = tables
        stats = sb("stats", [P, TB, 6])
        mv = sb("mv", [P, TB, 2])
        var, std, rough, newt, rstd = (sb(n, [P, TB]) for n in ("var", "std", "rough", "newt", "rstd"))

        def last(k):
            return w_all[:, k * TB * H:(k + 1) * TB * H]
        accs_l = [[last((ACCS + 2) * k + n) for k in range(LAST_RING)] for n in range(ACCS)]
        g_l, o_l = ([last((ACCS + 2) * k + ACCS + n) for k in range(LAST_RING)] for n in range(2))

        ps = ctx.enter_context(nc.psum_tensor("ps", [P, 8, 512], F32))

        s_waited_dve, s_waited_pool, s_waited_sp = (sem(f"s_waited_{e}") for e in ("dve", "pool", "sp"))
        s_const = sem("s_const")
        s_w = sem("s_w")
        s_gw = sem("s_gw")
        s_wexp = sem("s_wexp")
        s_x = sems("s_x", B)
        s_stats = sem("s_stats")
        s_ln = sem("s_ln")
        s_var = sem("s_var")
        s_std = sem("s_std")
        s_xn = sem("s_xn")
        s_rows = sems("s_rows", 2)
        s_xt_ps = sem("s_xt_ps")
        s_xt = sem("s_xt")
        s_lg_ps = sem("s_lg_ps")
        s_lg = sem("s_lg")
        s_chain = sem("s_chain")
        s_shift = sem("s_shift")
        s_exp = sem("s_exp")
        s_sel = sem("s_sel")
        s_cnt = sem("s_cnt")
        s_pos = sem("s_pos")
        s_extra = sem("s_extra")
        s_table = sem("s_table")
        s_table_d = sem("s_table_d")
        s_tables = sem("s_tables")
        s_pads = sem("s_pads")
        s_disp = sems("s_disp", 2)
        s_g_ps, s_a_ps, s_s_ps, s_r_ps, s_m_ps = (sem(f"s_{n}_ps") for n in "gasrm")
        s_g, s_a, s_p, s_r, s_m = (sem(f"s_{n}") for n in "gaprm")
        s_ab_ps = sem("s_ab_ps")
        s_silu = sem("s_silu")
        s_h = sem("s_h")
        s_y_ps = sem("s_y_ps")
        s_y = sem("s_y")
        s_at_ps = sem("s_at_ps")
        s_at = sem("s_at")
        s_mx = sem("s_mx")
        s_nmx = sem("s_nmx")
        s_ex = sem("s_ex")
        s_ri = sem("s_ri")
        s_acc0 = sems("s_acc0", 2)
        s_zero = sem("s_zero")
        s_slot = sems("s_slot", SLOT_RING)
        s_eT_ps, s_eab_ps, s_ehT_ps, s_ey_ps = (sem(n) for n in ("s_eT_ps", "s_eab_ps", "s_ehT_ps", "s_ey_ps"))
        s_eT, s_esilu, s_eh, s_ehT, s_ey = (sem(n) for n in ("s_eT", "s_esilu", "s_eh", "s_ehT", "s_ey"))
        s_add = sems("s_add", SLOT_RING)
        s_xl = sem("s_xl")
        s_fin = sems("s_fin", LAST_RING)
        s_sum, s_gate, s_sg, s_o = (sem(n) for n in ("s_sum", "s_gate", "s_sg", "s_o"))
        s_out = sems("s_out", LAST_RING)

        block = ctx.enter_context(nc.Block())
        ENG = mybir.EngineType

        @block.sync
        def _(sp):
            for b in range(B):
                sp.dma_start(s_all[:, b * TB * H:(b + 1) * TB * H].rearrange("p (t c) -> p t c", c=H),
                             x_b[b]).then_inc(s_x[b], 16)

            def rows(b):
                sp.wait_ge(s_xn, b.n * TB + TB)
                settle(sp, s_waited_sp, b)
                if b.behind(2):
                    sp.wait_ge(s_disp[b.slot], b.rounds(16 * TB * TOP_K))
                sp.dma_start(disp[b.slot][:, :, 0:H], xn[b.slot]).then_inc(s_rows[b.slot], 16)
            rolled(sp, B, 2, 2, rows)

            sp.wait_ge(s_table, 1)
            with nc.allow_non_contiguous_dma(reason="three small tables"):
                for k in range(3):
                    sp.dma_start(table_d[k].rearrange("(c p) -> p c", p=P), table[:, k, :]).then_inc(s_table_d, 16)
            sp.wait_ge(s_table_d, 48)
            for k in range(3):
                sp.dma_start(tables[k][:, 1:1 + 2 * P], table_d[k:k + 1, :]).then_inc(s_tables, 16)
            sp.wait_ge(s_tables, 48)

            for k in range(2):
                sp.wait_ge(s_disp[k], 16 * TOP_K * TILES // 2)
            sp.wait_ge(s_pads, 32)
            sp.wait_ge(s_at, 2 * B)
            for k in range(2):
                sp.wait_ge(s_acc0[k], 16 * (B // 2))

            def load_slots(t, row):
                if t.behind(SLOT_RING):
                    sp.wait_ge(s_add[t.slot], t.rounds(16))
                sp.dma_start(slot[:, t.slot, :], slots_d[bass.ds(row, P), :]).then_inc(s_slot[t.slot], 16)

            def round_of_slots(base):
                for c, row in enumerate(registers(nc, ENG.SP, w_row, base, SLOT_RING, SLOTS - P)):
                    load_slots(Item(base, c, SLOT_RING), row)
            round_of_slots(0)
            sp.dma_start(x_last.rearrange("p (b t c) -> p b t c", t=TB, c=H),
                         x.rearrange("(b t p) c -> p b t c", t=TB, p=P)).then_inc(s_xl, 16)
            with sp.Fori(1, SLOT_TILES // SLOT_RING) as r:
                round_of_slots(r * SLOT_RING)

            for k in range(SLOT_RING):
                sp.wait_ge(s_add[k], 16 * (SLOT_TILES // SLOT_RING))

            def load_last(b):
                for dst, src in zip(accs_l, acc_b):
                    sp.dma_start(dst[b.slot].rearrange("p (t c) -> p t c", c=H), src[b.n]).then_inc(s_fin[b.slot], 16)

            def store_out(b):
                sp.wait_ge(s_o, b.n + 1)
                sp.dma_start(out_b[b.n], o_l[b.slot].rearrange("p (t c) -> p t c", c=H)).then_inc(s_out[b.slot], 16)
            for c in range(LAST_RING):
                load_last(Item(0, c, LAST_RING))
            for c in range(B - LAST_RING):
                sp.wait_ge(s_gate, c + 1)
                load_last(Item(0, c + LAST_RING, LAST_RING))
                store_out(Item(0, c, LAST_RING))
            for c in range(B - LAST_RING, B):
                store_out(Item(0, c, LAST_RING))
            for k in range(LAST_RING):
                sp.wait_ge(s_out[k], 16 * (B // LAST_RING))

        @block.gpsimd
        def _(pool):
            pool.memset(ident[:], 0.0).then_inc(s_const, 1)
            pool.memset(pad[:], 0.0).then_inc(s_const, 1)
            pool.memset(tri[:], 1.0).then_inc(s_const, 1)
            pool.memset(ones[:], 1.0).then_inc(s_const, 1)
            for k in range(2):
                pool.memset(disp[k][:, :, C_TOKEN:ROW], 0.0).then_inc(s_const, 1)
            for r in (restart, restart4, restart8):
                pool.memset(r[:], 1.0).then_inc(s_const, 1)
            pool.iota(token_i[:], pattern=[[P, TB]], base=0, channel_multiplier=1).then_inc(s_const, 1)
            pool.iota(tile_i[:], pattern=[[P, 2]], base=0, channel_multiplier=1).then_inc(s_const, 1)
            pool.iota(first_i[:], pattern=[[REGION, E]], base=P + 1, channel_multiplier=0).then_inc(s_const, 1)
            pool.wait_ge(s_const, 12)
            pool.affine_select(out=ident[:], in_=ident[:], compare_op=ALU.not_equal, fill=1.0,
                               base=0, pattern=[[-1, P]], channel_multiplier=1).then_inc(s_const, 1)
            pool.iota(pad[:, C_TOKEN:C_TOKEN + 1].bitcast(I32), pattern=[[0, 1]], base=T, channel_multiplier=1).then_inc(s_const, 1)
            pool.affine_select(out=tri[:], in_=tri[:], compare_op=ALU.is_gt, fill=0.0,
                               base=0, pattern=[[1, P]], channel_multiplier=-1).then_inc(s_const, 1)
            for r, n in ((restart, E), (restart4, TB), (restart8, GROUPS)):
                pool.memset(r[:].rearrange("p (t e) -> p t e", e=n)[:, :, 0:1], 0.0).then_inc(s_const, 1)

            def scatter_rows(b):
                pool.wait_ge(s_rows[b.slot], b.rounds(16) + 16)
                pool.wait_ge(s_extra, b.n + 1)
                settle(pool, s_waited_pool, b)
                for t in range(TB):
                    for k in range(TOP_K):
                        at = disp[b.slot][:, t, C_SLOT + k:C_SLOT + k + 1].bitcast(I32)
                        pool.indirect_dma_start(slots_d[:, :], bass.IndirectOffsetOnAxis(ap=at, axis=0),
                                                disp[b.slot][:, t, :], None, bounds_check=SLOTS - 1,
                                                oob_is_err=False).then_inc(s_disp[b.slot], 16)
            rolled(pool, B, 2, 0, scatter_rows)

            pool.wait_ge(s_zero, 16 * ACCS)

            def add_rows(t):
                if t.behind(ACCS):
                    pool.wait_ge(s_add[(t.slot - ACCS) % SLOT_RING], t.rounds(16, back=ACCS) + 16)
                pool.wait_ge(s_ey, t.n + 1)
                settle(pool, s_waited_pool, t)
                to = slot[:, t.slot, C_TOKEN:C_TOKEN + 1].bitcast(I32)
                pool.indirect_dma_start(acc_d[t.slot % ACCS][:, :], bass.IndirectOffsetOnAxis(ap=to, axis=0),
                                        y_e[:, t.slot, :], None, bounds_check=T + P - 1, oob_is_err=False,
                                        compute_op=ALU.add).then_inc(s_add[t.slot], 16)
            rolled(pool, SLOT_TILES, SLOT_RING, SLOT_RING, add_rows)

            def gate(b):
                pool.wait_ge(s_gate, b.n + 1)
                pool.tensor_tensor(g_l[b.slot], g_l[b.slot], s_all[:, bass.ds(b.n * (TB * H), TB * H)],
                                   ALU.mult).then_inc(s_sg, 1)
            rolled(pool, B, LAST_RING, 0, gate)

        @block.scalar
        def _(act):
            act.dma_start(g_w[:], gwT.rearrange("(c p) n -> p c n", p=P)).then_inc(s_gw, 16)
            act.dma_start(sw13[:], sw13T.rearrange("w (c p) n -> p w c n", p=P)).then_inc(s_w, 16)
            for dst, src in ((w_k, wk), (w_q, wq), (sw2, sw2T), (w_o, wo), (w_vT, wvT)):
                act.dma_start(dst, src.rearrange("(c p) n -> p c n", p=P)).then_inc(s_w, 16)

            def root(b):
                act.wait_ge(s_var, b.n + 1)
                act.activation(std[:], var[:], ACT.Sqrt).then_inc(s_std, 1)

            def turned(b):
                for n in range(2):
                    act.wait_ge(s_xt_ps, b.n * 2 + n + 1)
                    act.activation(xnT[b.slot][:, :, 2 * n * P:(2 * n + 2) * P].rearrange("p c (t n) -> p t c n", t=2),
                                   ps[:, 2 + n, :].rearrange("p (t c n) -> p t c n", t=2, c=HC), ACT.Copy).then_inc(s_xt, 1)
                act.wait_ge(s_lg_ps, b.n + 1)
                if b.behind(1):
                    act.wait_ge(s_shift, b.n)
                act.activation(logits, ps[:, 4, 0:full], ACT.Copy).then_inc(s_lg, 1)

            def batch(b, turn=True, normal=True):
                act.wait_ge(s_shift, b.n + 1)
                act.activation(expd, shifted, ACT.Exp).then_inc(s_exp, 1)
                act.dma_start(w_all[:, bass.ds(b.n * W_STEP, W_STEP)],
                              wexp[:, bass.ds(b.n * W_STEP, W_STEP)]).then_inc(s_wexp, 16)
                act.wait_ge(s_g_ps, b.n + 1)
                act.activation(g_s, chunks(ps[:, 0, :]), ACT.Copy).then_inc(s_g, 1)
                for m in range(HC):
                    act.wait_ge(s_ab_ps, b.n * HC + m + 1)
                    act.activation(silu_s[m], ps[:, 4 + 2 * m, :], ACT.Silu).then_inc(s_silu, 1)
                if turn:
                    turned(Item(b.base, b.c + 1, 2))
                act.wait_ge(s_nmx, b.n + 1)
                for c in range(HC):
                    act.activation(p_s[:, c, :], ps[:, 0, c * H:(c + 1) * H], ACT.Exp, bias=nmx[:, c:c + 1],
                                   scale=SCALE, accum_out=rsum[:, c:c + 1]).then_inc(s_ex, 1)
                for n in range(2):
                    if n == 0 and b.behind(2):
                        act.wait_ge(s_acc0[b.slot], b.rounds(16))
                    act.wait_ge(s_y_ps, b.n * 2 + n + 1)
                    act.activation(y_s[b.slot][:, 2 * n:2 * n + 2, :],
                                   ps[:, 6 + n, :].rearrange("p (t c) -> p t c", c=H), ACT.Copy).then_inc(s_y, 1)
                act.wait_ge(s_r_ps, b.n + 1)
                act.activation(r_s, chunks(ps[:, 1, :]), ACT.Copy).then_inc(s_r, 1)
                act.wait_ge(s_y, b.n * 2 + 2)
                act.dma_start(acc_b[0][b.n], y_s[b.slot]).then_inc(s_acc0[b.slot], 16)
                if normal:
                    root(Item(b.base, b.c + 2, 2))

            root(Item(0, 0, 2))
            root(Item(0, 1, 2))
            turned(Item(0, 0, 2))
            act.wait_ge(s_const, 18)
            act.dma_start(acc_d[0][T:, :], pad[:, 0:H]).then_inc(s_zero, 16)
            act.dma_start(slots_d[E * REGION:, :], pad[:]).then_inc(s_pads, 16)
            batch(Item(0, 0, 2))
            act.dma_start(slots_d[0:E * REGION, :].rearrange("(e r) c -> r e c", r=REGION)[0:P],
                          pad[:].unsqueeze(1).to_broadcast([P, E, ROW])).then_inc(s_pads, 16)
            batch(Item(0, 1, 2))
            for a in acc_d[1:]:
                act.dma_start(a.rearrange("(t p) c -> p t c", p=P),
                              pad[:, 0:H].unsqueeze(1).to_broadcast([P, TILES + 1, H])).then_inc(s_zero, 16)
            with act.Fori(1, (B - 2) // 2) as r:
                for c in range(2):
                    batch(Item(r * 2, c, 2))
            batch(Item(0, B - 2, 2), normal=False)
            batch(Item(0, B - 1, 2), turn=False, normal=False)
            act.wait_ge(s_table, 1)
            act.dma_start(w_all[:, w_early:], wexp[:, w_early:]).then_inc(s_wexp, 16)

            act.wait_ge(s_tables, 48)

            def silu(t):
                if t.behind(2):
                    act.wait_ge(s_eh, t.n - 1)
                act.wait_ge(s_eab_ps, t.n + 1)
                act.activation(silu_e[t.slot % 2], ps[:, 2 + t.slot % 2, 0:I], ACT.Silu).then_inc(s_esilu, 1)

            def turned_hidden(t):
                act.wait_ge(s_ehT_ps, t.n + 1)
                act.activation(hT_e[t.slot % 2], ps[:, 4 + t.slot % 2, 0:P], ACT.Copy).then_inc(s_ehT, 1)

            def weigh(t):
                column = t.number()
                if t.behind(SLOT_RING):
                    act.wait_ge(s_add[t.slot], t.rounds(16))
                act.wait_ge(s_ey_ps, t.n + 1)
                act.activation(y_e[:, t.slot, :], ps[:, 6 + t.slot % 2, 0:H], ACT.Copy,
                               scale=slot[:, t.slot, bass.ds(column + C_WEIGHT, 1)]).then_inc(s_ey, 1)
            skewed(act, SLOT_TILES, [(silu, 1), (turned_hidden, 0), (weigh, -1)],
                   lambda at, n: registers(nc, ENG.Activation, w_col, at, n, E - 1))

            def gate(b):
                act.wait_ge(s_sum, b.n * (ACCS - 1) + ACCS - 1)
                if b.behind(LAST_RING):
                    act.wait_ge(s_o, b.n - LAST_RING + 1)
                act.activation(g_l[b.slot], accs_l[0][b.slot], ACT.Silu).then_inc(s_gate, 1)
            rolled(act, B, LAST_RING, LAST_RING, gate)

        @block.tensor
        def _(pe):
            pe.wait_ge(s_const, 18)
            pe.wait_ge(s_gw, 16)

            def turn(b):
                for n in range(2):
                    pe.wait_ge(s_xn, b.n * TB + 2 * n + 2)
                    if n == 1 and b.behind(1):
                        pe.wait_ge(s_pos, b.n)
                    for t in range(2):
                        for c in range(HC):
                            mm = pe.transpose(ps[:, 2 + n, (t * HC + c) * P:(t * HC + c + 1) * P],
                                              xn[b.slot][:, 2 * n + t, c * P:(c + 1) * P], ident[:])
                    mm.then_inc(s_xt_ps, 1)
                if b.behind(1):
                    pe.wait_ge(s_h, b.n * HC - 1)
                for t in range(TB):
                    if t % 2 == 0:
                        pe.wait_ge(s_xt, b.n * 2 + t // 2 + 1)
                    for c in range(HC):
                        mm = pe.matmul(ps[:, 4, t * E:(t + 1) * E], xnT[b.slot][:, c, t * P:(t + 1) * P],
                                       g_w[:, c, :], start=(c == 0), stop=(c == HC - 1))
                mm.then_inc(s_lg_ps, 1)

            def product(bank, lhs, rhs, done):
                for m in range(HC):
                    for k in range(HC):
                        mm = pe.matmul(ps[:, bank, m * H:(m + 1) * H], lhs[:, k, m * P:(m + 1) * P], rhs[:, k, :],
                                       start=(k == 0), stop=(k == HC - 1))
                mm.then_inc(done, 1)

            def shared_up(b, m):
                for w in range(2):
                    for k in range(HC):
                        mm = pe.matmul(ps[:, 4 + 2 * m + w, :], sw13[:, w, k, m * P:(m + 1) * P], xnT[b.slot][:, k, :],
                                       start=(k == 0), stop=(k == HC - 1))
                mm.then_inc(s_ab_ps, 1)

            def by_tile(b, bank, lhs, rhs, done):
                for n in range(2):
                    for t in range(2):
                        for k in range(HC):
                            at = (2 * n + t) * P
                            mm = pe.matmul(ps[:, bank + n, t * H:(t + 1) * H], lhs[:, k, at:at + P], rhs[:, k, :],
                                           start=(k == 0), stop=(k == HC - 1))
                    mm.then_inc(done, 1)

            def batch(b, more=True):
                xb = xn[b.slot]
                if b.behind(1):
                    pe.wait_ge(s_m, b.n)
                for m in range(HC):
                    for t in range(TB):
                        mm = pe.matmul(ps[:, 0, m * H:(m + 1) * H], xb[:, t, m * P:(m + 1) * P], xb[:, t, :],
                                       start=(t == 0), stop=(t == TB - 1))
                mm.then_inc(s_g_ps, 1)
                pe.wait_ge(s_lg, b.n + 1)
                shared_up(b, 0)
                pe.wait_ge(s_g, b.n + 1)
                if b.behind(1):
                    pe.wait_ge(s_r, b.n)
                product(1, g_s, w_k, s_a_ps)
                pe.wait_ge(s_sel, b.n + 1)
                if b.behind(1):
                    pe.wait_ge(s_at, b.n * 2)
                pe.matmul(ps[:, 3, 0:full], ones[:], sel16[:], start=True, stop=True)
                pe.matmul(ps[:, 3, full:2 * full], tri[:], sel16[:], start=True, stop=True).then_inc(s_cnt, 1)
                if b.behind(1):
                    pe.wait_ge(s_y, b.n * 2)
                shared_up(b, 1)
                pe.wait_ge(s_a, b.n + 1)
                product(0, w_q, a_s, s_s_ps)
                if more:
                    turn(Item(b.base, b.c + 1, 2))
                pe.wait_ge(s_h, b.n * HC + HC)
                by_tile(b, 6, hT_s, sw2, s_y_ps)
                pe.wait_ge(s_p, b.n * HC + HC)
                product(1, p_s, w_o, s_r_ps)
                pe.wait_ge(s_r, b.n + 1)
                product(0, w_vT, r_s, s_m_ps)
                pe.wait_ge(s_m, b.n + 1)
                if more:
                    pe.wait_ge(s_xt, b.n * 2 + 4)
                else:
                    pe.wait_ge(s_pos, b.n + 1)
                by_tile(b, 2, xnT[b.slot], m_s, s_at_ps)

            turn(Item(0, 0, 2))
            pe.wait_ge(s_w, 16 * 6)
            batch(Item(0, 0, 2))
            batch(Item(0, 1, 2))
            with pe.Fori(1, (B - 2) // 2) as r:
                for c in range(2):
                    batch(Item(r * 2, c, 2))
            batch(Item(0, B - 2, 2))
            batch(Item(0, B - 1, 2), more=False)

            pe.wait_ge(s_tables, 48)
            pe.wait_ge(s_wexp, 16 * (B + 1))
            pe.wait_ge(s_at, 2 * B)
            pe.wait_ge(s_y, 2 * B)

            def turn_rows(t):
                pe.wait_ge(s_slot[t.slot], t.rounds(16) + 16)
                if t.behind(2):
                    pe.wait_ge(s_eT, t.n - 1)
                for c in range(HC):
                    mm = pe.transpose(ps[:, t.slot % 2, c * P:(c + 1) * P], slot[:, t.slot, c * P:(c + 1) * P], ident[:])
                mm.then_inc(s_eT_ps, 1)

            def hidden(t):
                off = t.number()
                pe.wait_ge(s_eT, t.n + 1)
                if t.behind(2):
                    pe.wait_ge(s_eh, t.n - 1)
                for k in range(HC):
                    mm = pe.matmul(ps[:, 2 + t.slot % 2, 0:2 * I], xT[t.slot % 2][:, k, :],
                                   w_all[:, bass.ds(off + k * 2 * I, 2 * I)], start=(k == 0), stop=(k == HC - 1))
                mm.then_inc(s_eab_ps, 1)

            def turn_hidden(t):
                pe.wait_ge(s_eh, t.n + 1)
                if t.behind(2):
                    pe.wait_ge(s_ehT, t.n - 1)
                pe.transpose(ps[:, 4 + t.slot % 2, 0:P], h_e[t.slot % 2], ident[:]).then_inc(s_ehT_ps, 1)

            def expert_out(t):
                off = t.number()
                pe.wait_ge(s_ehT, t.n + 1)
                if t.behind(2):
                    pe.wait_ge(s_ey, t.n - 1)
                pe.matmul(ps[:, 6 + t.slot % 2, 0:H], hT_e[t.slot % 2], w_all[:, bass.ds(off + HC * 2 * I, H)],
                          start=True, stop=True).then_inc(s_ey_ps, 1)
            skewed(pe, SLOT_TILES, [(turn_rows, 2), (hidden, 1), (turn_hidden, 0), (expert_out, -1)],
                   lambda at, n: registers(nc, ENG.PE, w_off, at, n, (E - 1) * WEXP))

        @block.vector
        def _(dve):
            LN_STEPS = 8
            LINKS = 36

            def normal(b, var_done=None):
                base = b.n * LN_STEPS
                xb = s_all[:, bass.ds(b.n * (TB * H), TB * H)]
                for t in range(TB):
                    dve.bn_stats(stats[:, t, :], s_all[:, bass.ds(b.n * (TB * H) + t * H, H)]).then_inc(s_stats, 1)
                dve.wait_ge(s_stats, b.n * TB + TB)
                settle(dve, s_waited_dve, b)
                for t in range(TB):
                    ins = dve.bn_aggr(mv[:, t, :], stats[:, t, :])
                ins.then_inc(s_ln, 1)
                dve.wait_ge(s_ln, base + 1)
                dve.tensor_scalar(var[:], mv[:, :, 1], EPS, None, ALU.add).then_inc(s_var, 1)

            def normal_end(b):
                base = b.n * LN_STEPS
                dve.wait_ge(s_std, b.n + 1)
                dve.reciprocal(rough[:], std[:]).then_inc(s_ln, 1)
                dve.wait_ge(s_ln, base + 2)
                dve.tensor_tensor(newt[:], rough[:], rough[:], ALU.mult).then_inc(s_ln, 1)
                dve.wait_ge(s_ln, base + 3)
                dve.tensor_tensor(newt[:], newt[:], var[:], ALU.mult).then_inc(s_ln, 1)
                dve.wait_ge(s_ln, base + 4)
                dve.tensor_scalar(newt[:], newt[:], -0.5, 1.5, ALU.mult, ALU.add).then_inc(s_ln, 1)
                dve.wait_ge(s_ln, base + 5)
                dve.tensor_tensor(rstd[:], rough[:], newt[:], ALU.mult).then_inc(s_ln, 3)
                dve.wait_ge(s_ln, base + LN_STEPS)
                if b.behind(2):
                    dve.wait_ge(s_rows[b.slot], b.rounds(16))
                    dve.wait_ge(s_g_ps, b.n - 1)
                for t in range(TB):
                    dve.tensor_scalar(xn[b.slot][:, t, :], s_all[:, bass.ds(b.n * (TB * H) + t * H, H)],
                                      mv[:, t, 0:1], rstd[:, t:t + 1], ALU.subtract, ALU.mult).then_inc(s_xn, 1)

            links = {"n": 0, "b": None}

            def then(ins):
                links["n"] += 1
                ins.then_inc(s_chain, 1)
                dve.wait_ge(s_chain, links["b"].n * LINKS + links["n"])

            def by(v, n):
                return v.rearrange("p (t e) -> p t e", e=n)

            def spread(v, n):
                return v.unsqueeze(2).to_broadcast([P, v.shape[1], n])

            def choose(vals, n, k, above, same, prefix, chosen, again):
                settle(dve, s_waited_dve, links["b"])
                for t in range(TB):
                    ins = dve.max(top8[:, t, :], vals[:, t * n:(t + 1) * n])
                then(ins)
                kth = top8[:, :, k - 1:k].to_broadcast([P, TB, n])
                dve.tensor_tensor(by(above, n), by(vals, n), kth, ALU.is_gt)
                then(dve.tensor_tensor(by(same, n), by(vals, n), kth, ALU.is_equal))
                dve.tensor_reduce(row1[:], by(above, n), AX_X, ALU.add)
                then(dve.tensor_tensor_scan(prefix, again, same, 0.0, ALU.mult, ALU.add))
                then(dve.tensor_tensor(by(prefix, n), by(prefix, n), spread(row1[:], n), ALU.add))
                then(dve.scalar_tensor_tensor(prefix, prefix, float(k), same, ALU.is_le, ALU.mult))
                then(dve.tensor_tensor(chosen, above, prefix, ALU.add))

            def route(b):
                links["n"], links["b"] = 0, b
                dve.wait_ge(s_lg, b.n + 1)
                then(dve.tensor_reduce(row1[:], by(logits, E), AX_X, ALU.max))
                dve.tensor_tensor(by(shifted, E), by(logits, E), spread(row1[:], E), ALU.subtract).then_inc(s_shift, 1)
                dve.wait_ge(s_exp, b.n + 1)
                then(dve.tensor_reduce(row2[:], by(expd, E), AX_X, ALU.add))
                then(dve.reciprocal(row3[:], row2[:]))
                then(dve.tensor_tensor(by(scores, E), by(expd, E), spread(row3[:], E), ALU.mult))
                then(dve.tensor_reduce(gs, scores.rearrange("p (n g) -> p n g", g=PER_GROUP), AX_X, ALU.max))
                choose(gs, GROUPS, TOP_GROUPS, ggt, geq, gpref, gsel, restart8[:])
                then(dve.tensor_tensor(masked.rearrange("p (n g) -> p n g", g=PER_GROUP),
                                       scores.rearrange("p (n g) -> p n g", g=PER_GROUP),
                                       gsel.unsqueeze(2).to_broadcast([P, gfull, PER_GROUP]), ALU.mult))
                choose(masked, E, TOP_K, gt, eq, pref, sel, restart[:])
                dve.tensor_copy(sel16[:], sel).then_inc(s_sel, 1)

            def place(b):
                et = "p (e t) -> p e t"
                dve.wait_ge(s_cnt, b.n + 1)
                then(dve.tensor_copy(cnt_et.rearrange("p (e t) -> p t e", t=TB), by(ps[:, 3, 0:full], E)))
                then(dve.tensor_tensor_scan(inc_et, restart4[:], cnt_et, 0.0, ALU.mult, ALU.add))
                then(dve.tensor_tensor(cnt_et, inc_et, cnt_et, ALU.subtract))
                then(dve.tensor_tensor(cnt_et.rearrange(et, t=TB), cnt_et.rearrange(et, t=TB), spread(first[:], TB), ALU.add))
                dve.tensor_tensor(first[:], first[:], inc_et.rearrange(et, t=TB)[:, :, TB - 1], ALU.add)
                ins = dve.tensor_tensor(by(pos, E), by(ps[:, 3, full:2 * full], E),
                                        cnt_et.rearrange("p (e t) -> p t e", t=TB), ALU.add)
                ins.then_inc(s_pos, 1)
                dve.wait_ge(s_pos, b.n + 1)
                then(dve.tensor_tensor(pos, pos, sel, ALU.mult))
                settle(dve, s_waited_dve, b)
                for t in range(TB):
                    ins = dve.max(top8[:, t, :], pos[:, t * E:(t + 1) * E])
                then(ins)
                if b.behind(2):
                    dve.wait_ge(s_disp[b.slot], b.rounds(16 * TB * TOP_K))
                d = disp[b.slot]
                dve.tensor_scalar(d[:, :, C_SLOT:C_SLOT + TOP_K].bitcast(I32), top8[:, :, 0:TOP_K], -1.0, None, ALU.add)
                dve.tensor_copy(d[:, :, C_TOKEN].bitcast(I32), token[:])
                then(dve.tensor_tensor(wts, masked, sel, ALU.mult))
                dve.tensor_scalar(token[:], token[:], float(S), None, ALU.add)
                then(dve.tensor_reduce(row1[:], by(wts, E), AX_X, ALU.add))
                then(dve.tensor_scalar(row2[:], row1[:], 1e-20, None, ALU.add))
                then(dve.reciprocal(row3[:], row2[:]))
                ins = dve.tensor_tensor(d[:, :, C_WEIGHT:C_WEIGHT + E], by(wts, E), spread(row3[:], E), ALU.mult)
                ins.then_inc(s_extra, 1)
                left = LINKS - links["n"]
                assert left > 0, links
                dve.tensor_copy(row2[:], row3[:]).then_inc(s_chain, left)

            def hidden(b, m):
                dve.wait_ge(s_silu, b.n * HC + m + 1)
                dve.tensor_tensor(hT_s[:, m, :], silu_s[m], ps[:, 5 + 2 * m, :], ALU.mult).then_inc(s_h, 1)

            def batch(b, more=True):
                route(b)
                hidden(b, 0)
                dve.wait_ge(s_a_ps, b.n + 1)
                dve.tensor_copy(a_s, chunks(ps[:, 1, :])).then_inc(s_a, 1)
                place(b)
                hidden(b, 1)
                dve.wait_ge(s_s_ps, b.n + 1)
                dve.tensor_reduce(mx[:], chunks(ps[:, 0, :]), AX_X, ALU.max).then_inc(s_mx, 1)
                dve.wait_ge(s_mx, b.n + 1)
                dve.tensor_scalar(nmx[:], mx[:], -SCALE, None, ALU.mult).then_inc(s_nmx, 1)
                dve.wait_ge(s_ex, b.n * HC + HC)
                dve.reciprocal(rinv[:], rsum[:]).then_inc(s_ri, 1)
                dve.wait_ge(s_ri, b.n + 1)
                for c in range(HC):
                    dve.tensor_scalar(p_s[:, c, :], p_s[:, c, :], rinv[:, c:c + 1], None, ALU.mult).then_inc(s_p, 1)
                if more:
                    normal(Item(b.base, b.c + 2, 2))
                dve.wait_ge(s_m_ps, b.n + 1)
                dve.tensor_copy(m_s, chunks(ps[:, 0, :])).then_inc(s_m, 1)
                if more:
                    normal_end(Item(b.base, b.c + 2, 2))
                for n in range(2):
                    dve.wait_ge(s_at_ps, b.n * 2 + n + 1)
                    dve.tensor_copy(s_all[:, bass.ds(b.n * (TB * H) + n * 2 * H, 2 * H)], ps[:, 2 + n, :]).then_inc(s_at, 1)

            for c in range(2):
                dve.wait_ge(s_x[c], 16)
                normal(Item(0, c, 2))
                normal_end(Item(0, c, 2))
            for c in range(2, B):
                dve.wait_ge(s_x[c], 16)
            dve.wait_ge(s_const, 18)
            dve.tensor_copy(tile_f[:], tile_i[:])
            dve.tensor_copy(token[:], token_i[:])
            dve.tensor_copy(first[:], first_i[:])
            batch(Item(0, 0, 2))
            batch(Item(0, 1, 2))
            with dve.Fori(1, (B - 2) // 2) as r:
                for c in range(2):
                    batch(Item(r * 2, c, 2))
            batch(Item(0, B - 2, 2), more=False)
            batch(Item(0, B - 1, 2), more=False)

            links["n"], links["b"] = 0, Item(0, B, 2)
            then(dve.tensor_copy(used[:], first_i[:]))
            then(dve.tensor_tensor(used[:], first[:], used[:], ALU.subtract))
            then(dve.tensor_scalar(padded_i[:], used[:], float(P - 1), None, ALU.add))
            then(dve.tensor_scalar(padded_i[:], padded_i[:], -P, None, ALU.bitwise_and))
            then(dve.tensor_copy(padded[:], padded_i[:]))
            then(dve.tensor_tensor_scan(ends[:], padded[:], padded[:], 0.0, ALU.add, ALU.bypass))
            then(dve.scalar_tensor_tensor(shift[:], first[:], -1.0, ends[:], ALU.add, ALU.subtract))
            then(dve.tensor_scalar(ends[:], ends[:], 1.0 / P, None, ALU.mult))
            dve.memset(jump[:, E - 1:E], float(SLOTS))
            then(dve.tensor_tensor(jump[:, 0:E - 1], shift[:, 1:E], shift[:, 0:E - 1], ALU.subtract))
            for c in range(2):
                ins = dve.tensor_scalar(pairs[:, c, :], ends[:], tile_f[:, c:c + 1], None, ALU.is_le)
            then(ins)
            dve.tensor_reduce(expert[:], pairs[:], AX_X, ALU.add)
            then(dve.tensor_tensor(jumps[:], pairs[:], jump[:].unsqueeze(1).to_broadcast([P, 2, E]), ALU.mult))
            then(dve.tensor_reduce(begin[:], jumps[:], AX_X, ALU.add))
            then(dve.scalar_tensor_tensor(begin[:], tile_f[:], float(P), begin[:], ALU.mult, ALU.add))
            then(dve.tensor_scalar(begin[:], begin[:], shift[:, 0:1], None, ALU.add))
            then(dve.tensor_scalar(expert[:], expert[:], float(E - 1), None, ALU.min))
            dve.tensor_scalar(table[:, 0, :], expert[:], float(WEXP), None, ALU.mult)
            dve.tensor_copy(table[:, 1, :], expert[:])
            dve.tensor_scalar(table[:, 2, :], begin[:], float(SLOTS - P), None, ALU.min).then_inc(s_table, 1)

            def turned_rows(t):
                dve.wait_ge(s_eT_ps, t.n + 1)
                if t.behind(2):
                    dve.wait_ge(s_eab_ps, t.n - 1)
                dve.tensor_copy(xT[t.slot % 2], chunks(ps[:, t.slot % 2, 0:H])).then_inc(s_eT, 1)

            def hidden_rows(t):
                dve.wait_ge(s_esilu, t.n + 1)
                if t.behind(2):
                    dve.wait_ge(s_ehT_ps, t.n - 1)
                dve.tensor_tensor(h_e[t.slot % 2], silu_e[t.slot % 2], ps[:, 2 + t.slot % 2, I:2 * I], ALU.mult).then_inc(s_eh, 1)
            skewed(dve, SLOT_TILES, [(turned_rows, 2), (hidden_rows, 1)])

            dve.wait_ge(s_xl, 16)

            def sum_y(b):
                dve.wait_ge(s_fin[b.slot], b.rounds(16 * ACCS) + 16 * ACCS)
                a = [v[b.slot] for v in accs_l]
                for k in range(1, ACCS):
                    dve.tensor_tensor(a[0], a[0], a[k], ALU.add).then_inc(s_sum, 1)
                    if k < ACCS - 1:
                        dve.wait_ge(s_sum, b.n * (ACCS - 1) + k)

            def finish(b):
                dve.wait_ge(s_sg, b.n + 1)
                if b.behind(LAST_RING):
                    dve.wait_ge(s_out[b.slot], b.rounds(16))
                dve.tensor_tensor(o_l[b.slot], g_l[b.slot], x_last[:, bass.ds(b.n * (TB * H), TB * H)], ALU.add).then_inc(s_o, 1)
            sum_y(Item(0, 0, LAST_RING))
            for c in range(B - 1):
                sum_y(Item(0, c + 1, LAST_RING))
                finish(Item(0, c, LAST_RING))
            finish(Item(0, B - 1, LAST_RING))


def kernel(L0_attn_x, L0_attn_Wq, L0_attn_Wk, L0_attn_Wv, L0_attn_Wo, L0_ffn_gate_weight, L0_ffn_w1, L0_ffn_w2,
           L0_ffn_w3, L0_ffn_sw1, L0_ffn_sw2, L0_ffn_sw3):
    import concourse.bacc as bacc
    from concourse.bass_utils import run_bass_kernel_spmd as run

    def lay(a):
        return np.ascontiguousarray(a)

    a = {
        "x": lay(np.asarray(L0_attn_x).reshape(T, H)),
        "wq": lay(np.asarray(L0_attn_Wq)),
        "wk": lay(np.asarray(L0_attn_Wk)),
        "wvT": lay(np.asarray(L0_attn_Wv).T),
        "wo": lay(np.asarray(L0_attn_Wo)),
        "gwT": lay(np.asarray(L0_ffn_gate_weight).T),
    }
    w13 = np.stack([np.asarray(L0_ffn_w1), np.asarray(L0_ffn_w3)])
    w13 = w13.reshape(2, E, I, HC, P).transpose(4, 1, 3, 0, 2).reshape(P, E, HC * 2 * I)
    w2 = np.asarray(L0_ffn_w2).transpose(2, 0, 1)
    a["wexp"] = lay(np.concatenate([w13, w2], axis=2).reshape(P, E * WEXP))
    a["sw13T"] = lay(np.stack([np.asarray(L0_ffn_sw1).T, np.asarray(L0_ffn_sw3).T]))
    a["sw2T"] = lay(np.asarray(L0_ffn_sw2).T)

    nc = bacc.Bacc("TRN2", target_bir_lowering=False, num_devices=1)
    aps = [nc.dram_tensor(f"in_{n}", v.shape, mybir.dt.from_np(v.dtype), kind="ExternalInput").ap() for n, v in a.items()]
    out = nc.dram_tensor("out", (T, H), F32, kind="ExternalOutput").ap()
    gated_attention_moe(nc, *aps, out)
    r = run(nc, [{f"in_{n}": v for n, v in a.items()}], core_ids=[0])
    return r.results[0]["out"].reshape(B, S, H)
```

```python
from contextlib import ExitStack

import numpy as np

import concourse.bass as bass
from concourse import mybir

ALU = mybir.AluOpType
ACT = mybir.ActivationFunctionType
F32 = mybir.dt.float32
BF16 = mybir.dt.bfloat16
F16 = mybir.dt.float16
I32 = mybir.dt.int32
AX_X = mybir.AxisListType.X

P = 128
B, S, H = 8, 512, 256
T = B * S
TILES = T // P
TB = S // P
HC = H // P
E, I, SI = 32, 128, 256
GROUPS, TOP_GROUPS, TOP_K = 8, 3, 6
PER_GROUP = E // GROUPS
HEAD_DIM = 8
SCALE = 1.0 / float(np.sqrt(HEAD_DIM))
EPS = 1e-5
REGION = P + T
SLOTS = E * REGION + P
EXTRA = 48
ROW = H + EXTRA
C_WEIGHT, C_TOKEN, C_SLOT = H, H + E, H + E + 1
LT = 2
LAST_ITEMS, LAST_RING = TILES // LT, 4
WEXP = HC * 2 * I + H
EB = E // B
X_UP, W_UP = 256.0, 64.0
PARTS = ((0, 0), (0, 1), (1, 0))
SLOT_RING = 12
OUT_RING = 6
ACCS = 3
SLOT_TILES = T * TOP_K // P + E


class Item:

    def __init__(self, round, c, unroll):
        self.round, self.c, self.unroll = round, c, unroll
        self.static = isinstance(round, int)
        self.n = round * unroll + c
        self.slot = c % unroll

    def rounds(self, each, back=0):
        return self.round * each + each * ((self.c - back) // self.unroll)

    def behind(self, k):
        return not self.static or self.n >= k


def settle(eng, waited, item):
    if not item.static:
        eng.sem_inc(waited, 1)


def rolled(eng, total, unroll, peel, body):
    for c in range(peel):
        body(Item(0, c, unroll))
    if peel < total:
        with eng.Fori(peel // unroll, total // unroll) as r:
            for c in range(unroll):
                body(Item(r, c, unroll))
    for c in range(total // unroll * unroll, total):
        body(Item(0, c, unroll))


def registers(nc, engine, table, at, n, most):
    return nc.values_load_multi_w_load_instructions(
        table[0:1, bass.ds(at + 1, n)], engines=[engine], min_val=0, max_val=most,
        skip_runtime_bounds_check_because="the tables' entries are bounded where they are computed")[1]


def skewed(eng, total, stages, numbers=None, loop_from=SLOT_RING, unroll=SLOT_RING):
    most = max(lead for _, lead in stages)
    least = min(lead for _, lead in stages)

    def step(round, c, loaded=None):
        for stage, lead in stages:
            if isinstance(round, int) and not 0 <= c + lead < total:
                continue
            item = Item(round, c + lead, unroll)
            if numbers:
                item.number = lambda v=loaded[c + lead - least]: v
            stage(item)

    loop_to = (total - most) // unroll * unroll

    def written_out(begin, end):
        for at in range(begin, end, unroll):
            n = min(unroll, end - at)
            loaded = {}
            if numbers:
                items = range(max(at + least, 0), at + n + most)
                loaded = dict(zip((i - least for i in items), numbers(items[0], len(items))))
            for c in range(at, at + n):
                step(0, c, loaded)

    written_out(-most, loop_from)
    with eng.Fori(loop_from // unroll, loop_to // unroll) as r:
        loaded = numbers(r * unroll + least, unroll + most - least) if numbers else None
        for c in range(unroll):
            step(r, c, loaded)
    written_out(loop_to, total - least)


def gated_attention_moe(nc, x, wq, wk, wvT, wo, gwT, wexp, sw13T, sw2T, out):
    with ExitStack() as ctx:
        def sb(name, shape, dt=F32):
            return ctx.enter_context(nc.sbuf_tensor(name, shape, dt))

        def sem(name):
            return ctx.enter_context(nc.semaphore(name))

        def sems(name, n):
            return [sem(f"{name}{i}") for i in range(n)]

        slots_d = nc.dram_tensor("slots_d", [SLOTS, ROW], F32).ap()
        table_d = nc.dram_tensor("table_d", [3, 2 * P], I32).ap()
        acc_d = [nc.dram_tensor(f"acc{k}_d", [T + P, H], F32).ap() for k in range(ACCS)]
        acc_b = [a[0:T].rearrange("(b t p) c -> b p t c", t=TB, p=P) for a in acc_d]
        x_b = x.rearrange("(b t p) c -> b p t c", t=TB, p=P)
        pads_b = slots_d[0:E * REGION].rearrange("(b e r) c -> b r e c", e=EB, r=REGION)[:, 0:P]
        acc_l = [a[0:T].rearrange("(b t p) c -> b p t c", t=LT, p=P) for a in acc_d]
        out_l = out.rearrange("(b t p) c -> b p t c", t=LT, p=P)

        w_all = sb("w_all", [P, E * WEXP])
        s_all = sb("s_all", [P, TILES * H])
        places = {"at": 0}
        early = sb("early", [P, 10272])

        def carve(n, dt=F32):
            places["at"] += n
            v = early[:, places["at"] - n:places["at"]]
            return v if dt == F32 else v.bitcast(dt)

        def chunks(v, c=HC):
            return v.rearrange("p (c n) -> p c n", c=c)

        disp, xn, xnT = zip(*[(chunks(carve(TB * ROW), TB), chunks(carve(TB * H), TB), chunks(carve(HC * S)))
                              for _ in range(2)])
        raw_last = early[:, 0:EB * WEXP]
        w_q, w_k, w_vT, w_o, sw2 = (chunks(carve(HC * H)) for _ in range(5))
        x_last = early[:, 0:TILES * H]
        sw13_raw = w_all[:, (E - 2) * WEXP:(E - 2) * WEXP + 2 * HC * SI]
        sw13 = sb("sw13", [P, 2, 2, HC, SI], F16)
        xnT16 = sb("xnT16", [P, 2, HC, S], F16)
        g_w = sb("g_w", [P, HC, E])
        pad = sb("pad", [P, ROW])
        ident = sb("ident", [P, P])
        tri = sb("tri", [P, P], BF16)
        ones = sb("ones", [P, P], BF16)
        work = sb("work", [P, 9 * 512 + 2 * 1024])

        def part(at, n, c=None):
            return chunks(work[:, at:at + n], c) if c else work[:, at:at + n]
        g_s, a_s, p_s, r_s, m_s = (part(512 * k, 512, HC) for k in range(5))
        silu_s = [part(2560 + 512 * k, 512) for k in range(2)]
        hT_s = part(3584, 1024, HC)
        y_s = [part(4608 + 1024 * k, 1024, TB) for k in range(2)]
        mx, nmx, rsum, rinv = (sb(n, [P, HC]) for n in ("mx", "nmx", "rsum", "rinv"))
        slot = part(0, SLOT_RING * ROW, SLOT_RING)
        at = SLOT_RING * ROW
        xT = [part(at + H * k, H).bitcast(F16).rearrange("p (s c n) -> p s c n", s=2, c=HC) for k in range(2)]
        at += 2 * H
        silu_e, h_e = ([part(at + (2 * n + k) * I, I) for k in range(2)] for n in range(2))
        at += 4 * I
        hT_e = [chunks(part(at + I * k, I).bitcast(F16), 2) for k in range(2)]
        at += 2 * I
        y_e = part(at, OUT_RING * H, OUT_RING)
        assert at + OUT_RING * H <= work.shape[1]
        w16 = w_all[:].bitcast(F16)
        full, gfull = TB * E, TB * GROUPS
        logits, shifted, scores, masked, gt, eq, pref, sel = (carve(full) for _ in range(8))
        gs, ggt, geq, gpref, gsel = (carve(gfull) for _ in range(5))
        expd = shifted
        cnt_et, inc_et, pos, wts = gt, eq, pref, scores
        sel16 = sb("sel16", [P, full], BF16)
        restart = sb("restart", [P, full])
        restart4 = sb("restart4", [P, full])
        restart8 = sb("restart8", [P, gfull])
        top8 = sb("top8", [P, TB, 8])
        row1, row2, row3 = (sb(n, [P, TB]) for n in ("row1", "row2", "row3"))
        token = sb("token", [P, TB])
        token_i = sb("token_i", [P, TB], I32)
        first_i = sb("first_i", [P, E], I32)
        first = sb("first", [P, E])
        ends, padded, shift, jump = (gt[:, k * E:(k + 1) * E] for k in range(4))
        used, padded_i = eq[:, 0:E], eq[:, E:2 * E].bitcast(I32)
        pairs, jumps = (chunks(pref[:, k * 2 * E:(k + 1) * 2 * E], 2) for k in range(2))
        tile_i = sb("tile_i", [P, 2], I32)
        tile_f = sb("tile_f", [P, 2])
        expert, begin = sb("expert", [P, 2]), sb("begin", [P, 2])
        table = sb("table", [P, 3, 2], I32)
        at = places["at"] - 3 * (8 + 2 * P)
        assert at >= TILES * H
        tables = [early[0:1, at + k * (8 + 2 * P):at + (k + 1) * (8 + 2 * P)].bitcast(I32) for k in range(3)]
        w_off, w_col, w_row = tables
        stats = sb("stats", [P, TB, 6])
        mv = sb("mv", [P, TB, 2])
        var, std, rough, newt, rstd = (sb(n, [P, TB]) for n in ("var", "std", "rough", "newt", "rstd"))

        def last(k):
            return w_all[:, k * LT * H:(k + 1) * LT * H]
        accs_l = [[last((ACCS + 2) * k + n) for k in range(LAST_RING)] for n in range(ACCS)]
        g_l, o_l = ([last((ACCS + 2) * k + ACCS + n) for k in range(LAST_RING)] for n in range(2))

        ps = ctx.enter_context(nc.psum_tensor("ps", [P, 8, 512], F32))

        s_waited_dve, s_waited_pool, s_waited_sp = (sem(f"s_waited_{e}") for e in ("dve", "pool", "sp"))
        s_const = sem("s_const")
        s_w = sem("s_w")
        s_gw = sem("s_gw")
        s_wexp = sem("s_wexp")
        s_wlast = sem("s_wlast")
        s_whi = sem("s_whi")
        s_wlo = sem("s_wlo")
        s_x = sems("s_x", B)
        s_stats = sem("s_stats")
        s_ln = sem("s_ln")
        s_var = sem("s_var")
        s_warm = sem("s_warm")
        s_std = sem("s_std")
        s_xn = sem("s_xn")
        s_rows = sems("s_rows", 2)
        s_xt_ps = sem("s_xt_ps")
        s_xt = sem("s_xt")
        s_xthi = sem("s_xthi")
        s_xtlo = sem("s_xtlo")
        s_sw_raw = sem("s_sw_raw")
        s_swhi, s_swlo = sem("s_swhi"), sem("s_swlo")
        s_lg_ps = sem("s_lg_ps")
        s_lg = sem("s_lg")
        s_chain = sem("s_chain")
        s_shift = sem("s_shift")
        s_exp = sem("s_exp")
        s_sel = sem("s_sel")
        s_cnt = sem("s_cnt")
        s_pos = sem("s_pos")
        s_extra = sem("s_extra")
        s_table = sem("s_table")
        s_table_d = sem("s_table_d")
        s_tables = sem("s_tables")
        s_pads = sem("s_pads")
        s_disp = sems("s_disp", 2)
        s_g_ps, s_a_ps, s_s_ps, s_r_ps, s_m_ps = (sem(f"s_{n}_ps") for n in "gasrm")
        s_g, s_a, s_p, s_r, s_m = (sem(f"s_{n}") for n in "gaprm")
        s_ab_ps = sem("s_ab_ps")
        s_silu = sem("s_silu")
        s_h = sem("s_h")
        s_y_ps = sem("s_y_ps")
        s_y = sem("s_y")
        s_at_ps = sem("s_at_ps")
        s_at = sem("s_at")
        s_mx = sem("s_mx")
        s_nmx = sem("s_nmx")
        s_ex = sem("s_ex")
        s_ri = sem("s_ri")
        s_acc0 = sems("s_acc0", 2)
        s_zero = sem("s_zero")
        s_slot = sems("s_slot", SLOT_RING)
        s_eT_ps, s_eab_ps, s_ehT_ps, s_ey_ps = (sem(n) for n in ("s_eT_ps", "s_eab_ps", "s_ehT_ps", "s_ey_ps"))
        s_eThi, s_eT, s_esilu, s_eh = (sem(n) for n in ("s_eThi", "s_eT", "s_esilu", "s_eh"))
        s_ehThi, s_ehT, s_ey = (sem(n) for n in ("s_ehThi", "s_ehT", "s_ey"))
        s_add = sems("s_add", SLOT_RING)
        s_xl = sem("s_xl")
        s_fin = sems("s_fin", LAST_RING)
        s_sum, s_gate, s_sg, s_o = (sem(n) for n in ("s_sum", "s_gate", "s_sg", "s_o"))
        s_out = sems("s_out", LAST_RING)

        def count_bank(b):
            return 2 if b.static and b.n == 0 else 5

        def turned_half(v, n):
            return v[:, :, 2 * n * P:(2 * n + 2) * P]

        def turned_psum(n):
            return chunks(ps[:, 2 + n, :])

        def weights_of(b, low):
            return w16[:, bass.ds(b.n * (EB * 2 * WEXP), EB * 2 * WEXP)].rearrange(
                "p (e c) -> p e c", e=EB)[:, :, low * WEXP:(low + 1) * WEXP]

        def raw_weights(b, last):
            v = raw_last if last else w_all[:, bass.ds((b.n + 1) * (EB * WEXP), EB * WEXP)]
            return v.rearrange("p (e c) -> p e c", e=EB)

        block = ctx.enter_context(nc.Block())
        ENG = mybir.EngineType

        @block.sync
        def _(sp):
            def load_x(b):
                sp.dma_start(s_all[:, b * TB * H:(b + 1) * TB * H].rearrange("p (t c) -> p t c", c=H),
                             x_b[b]).then_inc(s_x[b], 16)
            for b in range(2):
                load_x(b)
            for dst, src in ((w_k, wk), (w_q, wq), (sw2, sw2T), (w_o, wo), (w_vT, wvT)):
                sp.dma_start(dst, src.rearrange("(c p) n -> p c n", p=P)).then_inc(s_w, 16)
            for b in range(2, B):
                load_x(b)

            sp.wait_ge(s_const, 18)
            for a in acc_d:
                sp.dma_start(a[T:, :], pad[:, 0:H]).then_inc(s_zero, 16)
            sp.dma_start(slots_d[E * REGION:, :], pad[:]).then_inc(s_pads, 16)

            def rows(b):
                sp.wait_ge(s_xn, b.n * TB + TB)
                settle(sp, s_waited_sp, b)
                if b.behind(2):
                    sp.wait_ge(s_disp[b.slot], b.rounds(16 * TB * TOP_K))
                sp.dma_start(disp[b.slot][:, :, 0:H], xn[b.slot]).then_inc(s_rows[b.slot], 16)
                for a in acc_b[1:]:
                    sp.dma_start(a[b.n], pad[:, 0:H].unsqueeze(1).to_broadcast([P, TB, H])).then_inc(s_zero, 16)
                sp.dma_start(pads_b[b.n], pad[:].unsqueeze(1).to_broadcast([P, EB, ROW])).then_inc(s_pads, 16)
            rolled(sp, B, 2, 2, rows)

            sp.wait_ge(s_disp[0], 16 * TOP_K * TILES // 2)
            sp.wait_ge(s_at, 2 * (B - 1))
            sp.dma_start(raw_last, wexp[:, (B - 1) * EB * WEXP:]).then_inc(s_wlast, 16)

            sp.wait_ge(s_table, 1)
            with nc.allow_non_contiguous_dma(reason="three small tables"):
                for k in range(3):
                    sp.dma_start(table_d[k].rearrange("(c p) -> p c", p=P), table[:, k, :]).then_inc(s_table_d, 16)
            sp.wait_ge(s_table_d, 48)
            for k in range(3):
                sp.dma_start(tables[k][:, 1:1 + 2 * P], table_d[k:k + 1, :]).then_inc(s_tables, 16)
            sp.wait_ge(s_tables, 48)

            for k in range(2):
                sp.wait_ge(s_disp[k], 16 * TOP_K * TILES // 2)
            sp.wait_ge(s_pads, 16 * (1 + B))
            sp.wait_ge(s_at, 2 * B)
            for k in range(2):
                sp.wait_ge(s_acc0[k], 16 * (B // 2))

            def load_slots(t, row):
                if t.behind(SLOT_RING):
                    sp.wait_ge(s_add[t.slot], t.rounds(16))
                sp.dma_start(slot[:, t.slot, :], slots_d[bass.ds(row, P), :]).then_inc(s_slot[t.slot], 16)

            def round_of_slots(r, begin=0, n=SLOT_RING):
                for c, row in enumerate(registers(nc, ENG.SP, w_row, r * SLOT_RING + begin, n, SLOTS - P)):
                    load_slots(Item(r, begin + c, SLOT_RING), row)
            round_of_slots(0)
            sp.wait_ge(s_wlo, B)
            with sp.Fori(1, 1 + B) as r:
                round_of_slots(r)
                sp.dma_start(x_last[:, bass.ds((r - 1) * (TB * H), TB * H)].rearrange("p (t c) -> p t c", c=H),
                             x_b[r - 1]).then_inc(s_xl, 16)
            with sp.Fori(1 + B, SLOT_TILES // SLOT_RING) as r:
                round_of_slots(r)
            round_of_slots(0, SLOT_TILES // SLOT_RING * SLOT_RING, SLOT_TILES % SLOT_RING)

            for k in range(SLOT_RING):
                sp.wait_ge(s_add[k], 16 * len(range(k, SLOT_TILES, SLOT_RING)))

            def load_last(b):
                for dst, src in zip(accs_l, acc_l):
                    sp.dma_start(dst[b.slot].rearrange("p (t c) -> p t c", c=H), src[b.n]).then_inc(s_fin[b.slot], 16)

            def store_out(b):
                sp.wait_ge(s_o, b.n + 1)
                sp.dma_start(out_l[b.n], o_l[b.slot].rearrange("p (t c) -> p t c", c=H)).then_inc(s_out[b.slot], 16)
            for c in range(LAST_RING):
                load_last(Item(0, c, LAST_RING))
            with sp.Fori(0, LAST_ITEMS // LAST_RING - 1) as r:
                for c in range(LAST_RING):
                    sp.wait_ge(s_gate, r * LAST_RING + c + 1)
                    load_last(Item(r, c + LAST_RING, LAST_RING))
                    store_out(Item(r, c, LAST_RING))
            for c in range(LAST_ITEMS - LAST_RING, LAST_ITEMS):
                store_out(Item(0, c, LAST_RING))
            for k in range(LAST_RING):
                sp.wait_ge(s_out[k], 16 * (LAST_ITEMS // LAST_RING))

        @block.gpsimd
        def _(pool):
            pool.memset(ident[:], 0.0).then_inc(s_const, 1)
            pool.memset(pad[:], 0.0).then_inc(s_const, 1)
            pool.memset(tri[:], 1.0).then_inc(s_const, 1)
            pool.memset(ones[:], 1.0).then_inc(s_const, 1)
            for k in range(2):
                pool.memset(disp[k][:, :, C_TOKEN:ROW], 0.0).then_inc(s_const, 1)
            for r in (restart, restart4, restart8):
                pool.memset(r[:], 1.0).then_inc(s_const, 1)
            pool.iota(token_i[:], pattern=[[P, TB]], base=0, channel_multiplier=1).then_inc(s_const, 1)
            pool.iota(tile_i[:], pattern=[[P, 2]], base=0, channel_multiplier=1).then_inc(s_const, 1)
            pool.iota(first_i[:], pattern=[[REGION, E]], base=P + 1, channel_multiplier=0).then_inc(s_const, 1)
            pool.wait_ge(s_const, 12)
            pool.affine_select(out=ident[:], in_=ident[:], compare_op=ALU.not_equal, fill=1.0,
                               base=0, pattern=[[-1, P]], channel_multiplier=1).then_inc(s_const, 1)
            pool.iota(pad[:, C_TOKEN:C_TOKEN + 1].bitcast(I32), pattern=[[0, 1]], base=T, channel_multiplier=1).then_inc(s_const, 1)
            pool.affine_select(out=tri[:], in_=tri[:], compare_op=ALU.is_gt, fill=0.0,
                               base=0, pattern=[[1, P]], channel_multiplier=-1).then_inc(s_const, 1)
            for r, n in ((restart, E), (restart4, TB), (restart8, GROUPS)):
                pool.memset(r[:].rearrange("p (t e) -> p t e", e=n)[:, :, 0:1], 0.0).then_inc(s_const, 1)

            def scatter_rows(b):
                pool.wait_ge(s_rows[b.slot], b.rounds(16) + 16)
                pool.wait_ge(s_extra, b.n + 1)
                settle(pool, s_waited_pool, b)
                for t in range(TB):
                    for k in range(TOP_K):
                        at = disp[b.slot][:, t, C_SLOT + k:C_SLOT + k + 1].bitcast(I32)
                        pool.indirect_dma_start(slots_d[:, :], bass.IndirectOffsetOnAxis(ap=at, axis=0),
                                                disp[b.slot][:, t, :], None, bounds_check=SLOTS - 1,
                                                oob_is_err=False).then_inc(s_disp[b.slot], 16)
            rolled(pool, B, 2, 0, scatter_rows)

            pool.wait_ge(s_zero, 16 * (ACCS + (ACCS - 1) * B))

            def add_rows(t):
                if t.behind(ACCS):
                    pool.wait_ge(s_add[(t.slot - ACCS) % SLOT_RING], t.rounds(16, back=ACCS) + 16)
                pool.wait_ge(s_ey, t.n + 1)
                settle(pool, s_waited_pool, t)
                to = slot[:, t.slot, C_TOKEN:C_TOKEN + 1].bitcast(I32)
                pool.indirect_dma_start(acc_d[t.slot % ACCS][:, :], bass.IndirectOffsetOnAxis(ap=to, axis=0),
                                        y_e[:, t.slot % OUT_RING, :], None, bounds_check=T + P - 1, oob_is_err=False,
                                        compute_op=ALU.add).then_inc(s_add[t.slot], 16)
            rolled(pool, SLOT_TILES, SLOT_RING, SLOT_RING, add_rows)

            def gate(b):
                pool.wait_ge(s_gate, b.n + 1)
                pool.tensor_tensor(g_l[b.slot], g_l[b.slot], s_all[:, bass.ds(b.n * (LT * H), LT * H)],
                                   ALU.mult).then_inc(s_sg, 1)
            rolled(pool, LAST_ITEMS, LAST_RING, 0, gate)

        @block.scalar
        def _(act):
            act.dma_start(g_w[:], gwT.rearrange("(c p) n -> p c n", p=P)).then_inc(s_gw, 16)
            act.dma_start(sw13_raw.rearrange("p (w c n) -> p w c n", w=2, c=HC),
                          sw13T.rearrange("w (c p) n -> p w c n", p=P)).then_inc(s_sw_raw, 16)

            def root(b):
                act.wait_ge(s_var, b.n + 1)
                act.activation(std[:], var[:], ACT.Sqrt).then_inc(s_std, 1)

            def turned(b):
                for n in range(2):
                    act.wait_ge(s_xt_ps, b.n * 2 + n + 1)
                    act.activation(turned_half(xnT[b.slot], n), turned_psum(n), ACT.Copy).then_inc(s_xt, 1)

            def gate_scores(b):
                act.wait_ge(s_lg_ps, b.n + 1)
                if b.behind(1):
                    act.wait_ge(s_shift, b.n)
                act.activation(logits, ps[:, 4, 0:full], ACT.Copy).then_inc(s_lg, 1)
                for n in range(2):
                    act.activation(turned_half(xnT16[:, 0], n), turned_psum(n), ACT.Copy, scale=X_UP).then_inc(s_xthi, 1)
                act.wait_ge(s_shift, b.n + 1)
                act.activation(expd, shifted, ACT.Exp).then_inc(s_exp, 1)

            def high_weights(b, last):
                if last:
                    act.wait_ge(s_wlast, 16)
                else:
                    act.wait_ge(s_wexp, b.n * 16 + 16)
                if b.behind(1):
                    act.wait_ge(s_wlo, b.n)
                act.activation(weights_of(b, 0), raw_weights(b, last), ACT.Copy, scale=W_UP).then_inc(s_whi, 1)

            def gram(b):
                act.wait_ge(s_g_ps, b.n * HC + HC)
                act.activation(g_s, chunks(ps[:, 0, :]), ACT.Copy).then_inc(s_g, 1)

            def batch(b, normal=True, last=False):
                if not last:
                    act.dma_start(w_all[:, bass.ds((b.n + 1) * (EB * WEXP), EB * WEXP)],
                                  wexp[:, bass.ds(b.n * (EB * WEXP), EB * WEXP)]).then_inc(s_wexp, 16)
                act.wait_ge(s_a_ps, b.n + 1)
                act.activation(a_s, chunks(ps[:, 1, :]), ACT.Copy).then_inc(s_a, 1)
                act.wait_ge(s_ab_ps, b.n * HC + 1)
                act.activation(silu_s[0], ps[:, 4, :], ACT.Silu, scale=1.0 / (X_UP * W_UP)).then_inc(s_silu, 1)
                act.wait_ge(s_ab_ps, b.n * HC + 2)
                act.activation(silu_s[1], ps[:, 6, :], ACT.Silu, scale=1.0 / (X_UP * W_UP)).then_inc(s_silu, 1)
                if not last:
                    turned(Item(b.round, b.c + 1, 2))
                act.wait_ge(s_nmx, b.n + 1)
                for c in range(HC):
                    act.activation(p_s[:, c, :], ps[:, 0, c * H:(c + 1) * H], ACT.Exp, bias=nmx[:, c:c + 1],
                                   scale=SCALE, accum_out=rsum[:, c:c + 1]).then_inc(s_ex, 1)
                if last:
                    high_weights(b, last)
                else:
                    gate_scores(Item(b.round, b.c + 1, 2))
                for n in range(2):
                    if n == 0 and b.behind(2):
                        act.wait_ge(s_acc0[b.slot], b.rounds(16))
                    act.wait_ge(s_y_ps, b.n * 2 + n + 1)
                    act.activation(y_s[b.slot][:, 2 * n:2 * n + 2, :],
                                   ps[:, 6 + n, :].rearrange("p (t c) -> p t c", c=H), ACT.Copy).then_inc(s_y, 1)
                    if n == 0:
                        act.wait_ge(s_r_ps, b.n + 1)
                        act.activation(r_s, chunks(ps[:, 1, :]), ACT.Copy).then_inc(s_r, 1)
                act.wait_ge(s_y, b.n * 2 + 2)
                act.dma_start(acc_b[0][b.n], y_s[b.slot]).then_inc(s_acc0[b.slot], 16)
                act.wait_ge(s_m_ps, b.n + 1)
                act.activation(m_s, chunks(ps[:, 1, :]), ACT.Copy).then_inc(s_m, 1)
                if not last:
                    gram(Item(b.round, b.c + 1, 2))
                for n in range(2):
                    act.wait_ge(s_at_ps, b.n * 2 + n + 1)
                    act.activation(s_all[:, bass.ds(b.n * (TB * H) + n * 2 * H, 2 * H)], ps[:, 2 + n, :], ACT.Copy).then_inc(s_at, 1)
                if normal:
                    root(Item(b.round, b.c + 2, 2))
                if not last:
                    high_weights(b, last)

            act.wait_ge(s_const, 2)
            act.activation(std[:, 0:1], pad[:, 0:1], ACT.Sqrt).then_inc(s_warm, 1)
            act.wait_ge(s_warm, 1)
            root(Item(0, 0, 2))
            act.wait_ge(s_sw_raw, 16)
            act.activation(sw13[:, 0].rearrange("p w c n -> p (w c n)"), sw13_raw, ACT.Copy, scale=W_UP).then_inc(s_swhi, 1)
            turned(Item(0, 0, 2))
            root(Item(0, 1, 2))
            gate_scores(Item(0, 0, 2))
            gram(Item(0, 0, 2))
            batch(Item(0, 0, 2))
            batch(Item(0, 1, 2))
            with act.Fori(1, (B - 2) // 2) as r:
                for c in range(2):
                    batch(Item(r, c, 2))
            batch(Item(0, B - 2, 2), normal=False)
            batch(Item(0, B - 1, 2), normal=False, last=True)

            act.wait_ge(s_tables, 48)

            def high_rows(t):
                if t.behind(2):
                    act.wait_ge(s_eab_ps, t.n - 1)
                act.wait_ge(s_eT_ps, t.n + 1)
                act.activation(xT[t.slot % 2][:, 0], chunks(ps[:, t.slot % 2, 0:H]), ACT.Copy, scale=X_UP).then_inc(s_eThi, 1)

            def silu(t):
                if t.behind(2):
                    act.wait_ge(s_eh, t.n - 1)
                act.wait_ge(s_eab_ps, t.n + 1)
                act.activation(silu_e[t.slot % 2], ps[:, 2 + t.slot % 2, 0:I], ACT.Silu,
                               scale=1.0 / (X_UP * W_UP)).then_inc(s_esilu, 1)

            def turned_hidden(t):
                act.wait_ge(s_ehT_ps, t.n + 1)
                if t.behind(2):
                    act.wait_ge(s_ey_ps, t.n - 1)
                act.activation(hT_e[t.slot % 2][:, 0], ps[:, 4 + t.slot % 2, 0:P], ACT.Copy).then_inc(s_ehThi, 1)

            def weigh(t):
                column = t.number()
                if t.behind(OUT_RING):
                    act.wait_ge(s_add[(t.slot - OUT_RING) % SLOT_RING], t.rounds(16, back=OUT_RING) + 16)
                act.wait_ge(s_ey_ps, t.n + 1)
                act.activation(y_e[:, t.slot % OUT_RING, :], ps[:, 6 + t.slot % 2, 0:H], ACT.Copy,
                               scale=slot[:, t.slot, bass.ds(column + C_WEIGHT, 1)]).then_inc(s_ey, 1)
            skewed(act, SLOT_TILES, [(high_rows, 2), (silu, 1), (turned_hidden, 0), (weigh, -1)],
                   lambda at, n: registers(nc, ENG.Activation, w_col, at, n, E - 1))

            def gate(b):
                act.wait_ge(s_sum, b.n * (ACCS - 1) + ACCS - 1)
                if b.behind(LAST_RING):
                    act.wait_ge(s_o, b.n - LAST_RING + 1)
                act.activation(g_l[b.slot], accs_l[0][b.slot], ACT.Silu).then_inc(s_gate, 1)
            rolled(act, LAST_ITEMS, LAST_RING, LAST_RING, gate)

        @block.tensor
        def _(pe):
            pe.wait_ge(s_const, 18)
            pe.wait_ge(s_gw, 16)

            def turn(b):
                for n in range(2):
                    pe.wait_ge(s_xn, b.n * TB + 2 * n + 2)
                    if n == 0 and b.behind(2):
                        pe.wait_ge(s_at, b.n * 2 - 2)
                    elif n == 0 and b.behind(1):
                        pe.wait_ge(s_pos, 1)
                    for t in range(2):
                        for c in range(HC):
                            mm = pe.transpose(ps[:, 2 + n, (c * 2 + t) * P:(c * 2 + t + 1) * P],
                                              xn[b.slot][:, 2 * n + t, c * P:(c + 1) * P], ident[:])
                    mm.then_inc(s_xt_ps, 1)

            def gate(b):
                if b.behind(1):
                    pe.wait_ge(s_h, b.n * HC - 1)
                for t in range(TB):
                    if t % 2 == 0:
                        pe.wait_ge(s_xt, b.n * 2 + t // 2 + 1)
                    for c in range(HC):
                        mm = pe.matmul(ps[:, 4, t * E:(t + 1) * E], xnT[b.slot][:, c, t * P:(t + 1) * P],
                                       g_w[:, c, :], start=(c == 0), stop=(c == HC - 1))
                mm.then_inc(s_lg_ps, 1)

            def count(b):
                pe.wait_ge(s_sel, b.n + 1)
                pe.matmul(ps[:, count_bank(b), 0:full], ones[:], sel16[:], start=True, stop=True)
                pe.matmul(ps[:, count_bank(b), full:2 * full], tri[:], sel16[:], start=True, stop=True).then_inc(s_cnt, 1)

            def product(bank, lhs, rhs, done):
                for m in range(HC):
                    for k in range(HC):
                        mm = pe.matmul(ps[:, bank, m * H:(m + 1) * H], lhs[:, k, m * P:(m + 1) * P], rhs[:, k, :],
                                       start=(k == 0), stop=(k == HC - 1))
                mm.then_inc(done, 1)

            def shared_up(b, m):
                for w in range(2):
                    for n, (w_low, x_low) in enumerate(PARTS):
                        for k in range(HC):
                            mm = pe.matmul(ps[:, 4 + 2 * m + w, :], sw13[:, w_low, w, k, m * P:(m + 1) * P],
                                           xnT16[:, x_low, k, :], start=(n == 0 and k == 0), stop=(n == 2 and k == HC - 1))
                mm.then_inc(s_ab_ps, 1)

            def half_by_tile(n, bank, lhs, rhs, done):
                for t in range(2):
                    for k in range(HC):
                        at = (2 * n + t) * P
                        mm = pe.matmul(ps[:, bank + n, t * H:(t + 1) * H], lhs[:, k, at:at + P], rhs[:, k, :],
                                       start=(k == 0), stop=(k == HC - 1))
                mm.then_inc(done, 1)

            def gram(b, m):
                for t in range(TB):
                    mm = pe.matmul(ps[:, 0, m * H:(m + 1) * H], xn[b.slot][:, t, m * P:(m + 1) * P], xn[b.slot][:, t, :],
                                   start=(t == 0), stop=(t == TB - 1))
                mm.then_inc(s_g_ps, 1)

            def batch(b, last=False, first=False):
                nxt = Item(b.round, b.c + 1, 2)
                pe.wait_ge(s_lg, b.n + 1)
                if not first:
                    pe.wait_ge(s_pos, b.n + 1)
                pe.wait_ge(s_xtlo, b.n * 2 + 2)
                shared_up(b, 0)
                if first:
                    count(b)
                pe.wait_ge(s_g, b.n + 1)
                if b.behind(1):
                    pe.wait_ge(s_m, b.n)
                product(1, g_s, w_k, s_a_ps)
                if b.behind(1):
                    pe.wait_ge(s_y, b.n * 2)
                shared_up(b, 1)
                if not last:
                    turn(nxt)
                pe.wait_ge(s_a, b.n + 1)
                product(0, w_q, a_s, s_s_ps)
                if not last:
                    gate(nxt)
                pe.wait_ge(s_h, b.n * HC + HC)
                half_by_tile(0, 6, hT_s, sw2, s_y_ps)
                pe.wait_ge(s_p, b.n * HC + HC)
                product(1, p_s, w_o, s_r_ps)
                half_by_tile(1, 6, hT_s, sw2, s_y_ps)
                pe.wait_ge(s_r, b.n + 1)
                product(1, w_vT, r_s, s_m_ps)
                if not last:
                    gram(nxt, 0)
                    gram(nxt, 1)
                    count(nxt)
                pe.wait_ge(s_m, b.n + 1)
                if not last:
                    pe.wait_ge(s_xtlo, b.n * 2 + 4)
                else:
                    pe.wait_ge(s_at, b.n * 2)
                for n in range(2):
                    half_by_tile(n, 2, xnT[b.slot], m_s, s_at_ps)

            turn(Item(0, 0, 2))
            gate(Item(0, 0, 2))
            for m in range(HC):
                gram(Item(0, 0, 2), m)
            pe.wait_ge(s_w, 16 * 5)
            pe.wait_ge(s_swlo, 1)
            batch(Item(0, 0, 2), first=True)
            batch(Item(0, 1, 2))
            with pe.Fori(1, (B - 2) // 2) as r:
                for c in range(2):
                    batch(Item(r, c, 2))
            batch(Item(0, B - 2, 2))
            batch(Item(0, B - 1, 2), last=True)

            pe.wait_ge(s_tables, 48)
            pe.wait_ge(s_wlo, B)
            pe.wait_ge(s_at, 2 * B)
            pe.wait_ge(s_y, 2 * B)

            def turn_rows(t):
                pe.wait_ge(s_slot[t.slot], t.rounds(16) + 16)
                if t.behind(2):
                    pe.wait_ge(s_eT, t.n - 1)
                for c in range(HC):
                    mm = pe.transpose(ps[:, t.slot % 2, c * P:(c + 1) * P], slot[:, t.slot, c * P:(c + 1) * P], ident[:])
                mm.then_inc(s_eT_ps, 1)

            def hidden(t):
                off = t.number()
                pe.wait_ge(s_eT, t.n + 1)
                if t.behind(2):
                    pe.wait_ge(s_eh, t.n - 1)
                for n, (x_low, w_low) in enumerate(PARTS):
                    for k in range(HC):
                        mm = pe.matmul(ps[:, 2 + t.slot % 2, 0:2 * I], xT[t.slot % 2][:, x_low, k, :],
                                       w16[:, bass.ds(off + w_low * WEXP + k * 2 * I, 2 * I)],
                                       start=(n == 0 and k == 0), stop=(n == 2 and k == HC - 1))
                mm.then_inc(s_eab_ps, 1)

            def turn_hidden(t):
                pe.wait_ge(s_eh, t.n + 1)
                if t.behind(2):
                    pe.wait_ge(s_ehT, t.n - 1)
                pe.transpose(ps[:, 4 + t.slot % 2, 0:P], h_e[t.slot % 2], ident[:]).then_inc(s_ehT_ps, 1)

            def expert_out(t):
                off = t.number()
                pe.wait_ge(s_ehT, t.n + 1)
                if t.behind(2):
                    pe.wait_ge(s_ey, t.n - 1)
                for n, (h_low, w_low) in enumerate(PARTS):
                    mm = pe.matmul(ps[:, 6 + t.slot % 2, 0:H], hT_e[t.slot % 2][:, h_low],
                                   w16[:, bass.ds(off + w_low * WEXP + HC * 2 * I, H)], start=(n == 0), stop=(n == 2))
                mm.then_inc(s_ey_ps, 1)
            skewed(pe, SLOT_TILES, [(turn_rows, 2), (hidden, 1), (turn_hidden, 0), (expert_out, -1)],
                   lambda at, n: registers(nc, ENG.PE, w_off, at, n, (E - 1) * 2 * WEXP))

        @block.vector
        def _(dve):
            LN_STEPS = 8
            LINKS = 36

            def normal(b):
                base = b.n * LN_STEPS
                xb = s_all[:, bass.ds(b.n * (TB * H), TB * H)]
                for t in range(TB):
                    dve.bn_stats(stats[:, t, :], s_all[:, bass.ds(b.n * (TB * H) + t * H, H)]).then_inc(s_stats, 1)
                dve.wait_ge(s_stats, b.n * TB + TB)
                settle(dve, s_waited_dve, b)
                for t in range(TB):
                    ins = dve.bn_aggr(mv[:, t, :], stats[:, t, :])
                ins.then_inc(s_ln, 1)
                dve.wait_ge(s_ln, base + 1)
                dve.tensor_scalar(var[:], mv[:, :, 1], EPS, None, ALU.add).then_inc(s_var, 1)

            def normal_end(b):
                base = b.n * LN_STEPS
                dve.wait_ge(s_std, b.n + 1)
                dve.reciprocal(rough[:], std[:]).then_inc(s_ln, 1)
                dve.wait_ge(s_ln, base + 2)
                dve.tensor_tensor(newt[:], rough[:], rough[:], ALU.mult).then_inc(s_ln, 1)
                dve.wait_ge(s_ln, base + 3)
                dve.tensor_tensor(newt[:], newt[:], var[:], ALU.mult).then_inc(s_ln, 1)
                dve.wait_ge(s_ln, base + 4)
                dve.tensor_scalar(newt[:], newt[:], -0.5, 1.5, ALU.mult, ALU.add).then_inc(s_ln, 1)
                dve.wait_ge(s_ln, base + 5)
                dve.tensor_tensor(rstd[:], rough[:], newt[:], ALU.mult).then_inc(s_ln, 3)
                dve.wait_ge(s_ln, base + LN_STEPS)
                if b.behind(2):
                    dve.wait_ge(s_rows[b.slot], b.rounds(16))
                    dve.wait_ge(s_g_ps, b.n * HC - HC)
                for t in range(TB):
                    dve.tensor_scalar(xn[b.slot][:, t, :], s_all[:, bass.ds(b.n * (TB * H) + t * H, H)],
                                      mv[:, t, 0:1], rstd[:, t:t + 1], ALU.subtract, ALU.mult).then_inc(s_xn, 1)

            links = {"n": 0, "b": None}

            def then(ins):
                links["n"] += 1
                ins.then_inc(s_chain, 1)
                dve.wait_ge(s_chain, links["b"].n * LINKS + links["n"])

            def by(v, n):
                return v.rearrange("p (t e) -> p t e", e=n)

            def spread(v, n):
                return v.unsqueeze(2).to_broadcast([P, v.shape[1], n])

            def choose(vals, n, k, above, same, prefix, chosen, again):
                settle(dve, s_waited_dve, links["b"])
                for t in range(TB):
                    ins = dve.max(top8[:, t, :], vals[:, t * n:(t + 1) * n])
                then(ins)
                kth = top8[:, :, k - 1:k].to_broadcast([P, TB, n])
                dve.tensor_tensor(by(above, n), by(vals, n), kth, ALU.is_gt)
                then(dve.tensor_tensor(by(same, n), by(vals, n), kth, ALU.is_equal))
                dve.tensor_reduce(row1[:], by(above, n), AX_X, ALU.add)
                then(dve.tensor_tensor_scan(prefix, again, same, 0.0, ALU.mult, ALU.add))
                then(dve.tensor_tensor(by(prefix, n), by(prefix, n), spread(row1[:], n), ALU.add))
                then(dve.scalar_tensor_tensor(prefix, prefix, float(k), same, ALU.is_le, ALU.mult))
                then(dve.tensor_tensor(chosen, above, prefix, ALU.add))

            def route(b):
                links["n"], links["b"] = 0, b
                dve.wait_ge(s_lg, b.n + 1)
                then(dve.tensor_reduce(row1[:], by(logits, E), AX_X, ALU.max))
                dve.tensor_tensor(by(shifted, E), by(logits, E), spread(row1[:], E), ALU.subtract).then_inc(s_shift, 1)
                for n in range(2):
                    dve.wait_ge(s_xthi, b.n * 2 + n + 1)
                    dve.scalar_tensor_tensor(turned_half(xnT16[:, 1], n), turned_psum(n), X_UP, turned_half(xnT16[:, 0], n),
                                             ALU.mult, ALU.subtract).then_inc(s_xtlo, 1)
                dve.wait_ge(s_exp, b.n + 1)
                then(dve.tensor_reduce(row2[:], by(expd, E), AX_X, ALU.add))
                then(dve.reciprocal(row3[:], row2[:]))
                then(dve.tensor_tensor(by(scores, E), by(expd, E), spread(row3[:], E), ALU.mult))
                then(dve.tensor_reduce(gs, scores.rearrange("p (n g) -> p n g", g=PER_GROUP), AX_X, ALU.max))
                choose(gs, GROUPS, TOP_GROUPS, ggt, geq, gpref, gsel, restart8[:])
                then(dve.tensor_tensor(masked.rearrange("p (n g) -> p n g", g=PER_GROUP),
                                       scores.rearrange("p (n g) -> p n g", g=PER_GROUP),
                                       gsel.unsqueeze(2).to_broadcast([P, gfull, PER_GROUP]), ALU.mult))
                choose(masked, E, TOP_K, gt, eq, pref, sel, restart[:])
                dve.tensor_copy(sel16[:], sel).then_inc(s_sel, 1)

            def place(b):
                et = "p (e t) -> p e t"
                dve.wait_ge(s_cnt, b.n + 1)
                then(dve.tensor_copy(cnt_et.rearrange("p (e t) -> p t e", t=TB), by(ps[:, count_bank(b), 0:full], E)))
                then(dve.tensor_tensor_scan(inc_et, restart4[:], cnt_et, 0.0, ALU.mult, ALU.add))
                then(dve.tensor_tensor(cnt_et, inc_et, cnt_et, ALU.subtract))
                then(dve.tensor_tensor(cnt_et.rearrange(et, t=TB), cnt_et.rearrange(et, t=TB), spread(first[:], TB), ALU.add))
                dve.tensor_tensor(first[:], first[:], inc_et.rearrange(et, t=TB)[:, :, TB - 1], ALU.add)
                ins = dve.tensor_tensor(by(pos, E), by(ps[:, count_bank(b), full:2 * full], E),
                                        cnt_et.rearrange("p (e t) -> p t e", t=TB), ALU.add)
                ins.then_inc(s_pos, 1)
                dve.wait_ge(s_pos, b.n + 1)
                then(dve.tensor_tensor(pos, pos, sel, ALU.mult))
                settle(dve, s_waited_dve, b)
                for t in range(TB):
                    ins = dve.max(top8[:, t, :], pos[:, t * E:(t + 1) * E])
                then(ins)
                if b.behind(2):
                    dve.wait_ge(s_disp[b.slot], b.rounds(16 * TB * TOP_K))
                d = disp[b.slot]
                dve.tensor_scalar(d[:, :, C_SLOT:C_SLOT + TOP_K].bitcast(I32), top8[:, :, 0:TOP_K], -1.0, None, ALU.add)
                dve.tensor_copy(d[:, :, C_TOKEN].bitcast(I32), token[:])
                then(dve.tensor_tensor(wts, masked, sel, ALU.mult))
                dve.tensor_scalar(token[:], token[:], float(S), None, ALU.add)
                then(dve.tensor_reduce(row1[:], by(wts, E), AX_X, ALU.add))
                then(dve.tensor_scalar(row2[:], row1[:], 1e-20, W_UP, ALU.add, ALU.mult))
                then(dve.reciprocal(row3[:], row2[:]))
                ins = dve.tensor_tensor(d[:, :, C_WEIGHT:C_WEIGHT + E], by(wts, E), spread(row3[:], E), ALU.mult)
                ins.then_inc(s_extra, 1)
                left = LINKS - links["n"]
                assert left > 0, links
                dve.tensor_copy(row2[:], row3[:]).then_inc(s_chain, left)

            def hidden(b, m):
                dve.wait_ge(s_silu, b.n * HC + m + 1)
                dve.scalar_tensor_tensor(hT_s[:, m, :], ps[:, 5 + 2 * m, :], 1.0 / (X_UP * W_UP), silu_s[m],
                                         ALU.mult, ALU.mult).then_inc(s_h, 1)

            def low_weights(b, last):
                dve.wait_ge(s_whi, b.n + 1)
                dve.scalar_tensor_tensor(weights_of(b, 1), raw_weights(b, last), W_UP, weights_of(b, 0),
                                         ALU.mult, ALU.subtract).then_inc(s_wlo, 1)

            def batch(b, more=True, last=False):
                hidden(b, 0)
                hidden(b, 1)
                dve.wait_ge(s_s_ps, b.n + 1)
                dve.tensor_reduce(mx[:], chunks(ps[:, 0, :]), AX_X, ALU.max).then_inc(s_mx, 1)
                dve.wait_ge(s_mx, b.n + 1)
                dve.tensor_scalar(nmx[:], mx[:], -SCALE, None, ALU.mult).then_inc(s_nmx, 1)
                dve.wait_ge(s_ex, b.n * HC + HC)
                dve.reciprocal(rinv[:], rsum[:]).then_inc(s_ri, 1)
                dve.wait_ge(s_ri, b.n + 1)
                for c in range(HC):
                    dve.tensor_scalar(p_s[:, c, :], p_s[:, c, :], rinv[:, c:c + 1], None, ALU.mult).then_inc(s_p, 1)
                if not last:
                    route(Item(b.round, b.c + 1, 2))
                    place(Item(b.round, b.c + 1, 2))
                if more:
                    normal(Item(b.round, b.c + 2, 2))
                    normal_end(Item(b.round, b.c + 2, 2))
                elif not last:
                    slot_tiles()
                low_weights(b, last)

            def slot_tiles():
                links["n"], links["b"] = 0, Item(0, B, 2)
                then(dve.tensor_copy(used, first_i[:]))
                then(dve.tensor_tensor(used, first[:], used, ALU.subtract))
                then(dve.tensor_scalar(padded_i, used, float(P - 1), None, ALU.add))
                then(dve.tensor_scalar(padded_i, padded_i, -P, None, ALU.bitwise_and))
                then(dve.tensor_copy(padded, padded_i))
                then(dve.tensor_tensor_scan(ends, padded, padded, 0.0, ALU.add, ALU.bypass))
                then(dve.scalar_tensor_tensor(shift, first[:], -1.0, ends, ALU.add, ALU.subtract))
                then(dve.tensor_scalar(ends, ends, 1.0 / P, None, ALU.mult))
                dve.memset(jump[:, E - 1:E], float(SLOTS))
                then(dve.tensor_tensor(jump[:, 0:E - 1], shift[:, 1:E], shift[:, 0:E - 1], ALU.subtract))
                for c in range(2):
                    ins = dve.tensor_scalar(pairs[:, c, :], ends, tile_f[:, c:c + 1], None, ALU.is_le)
                then(ins)
                dve.tensor_reduce(expert[:], pairs, AX_X, ALU.add)
                then(dve.tensor_tensor(jumps, pairs, jump.unsqueeze(1).to_broadcast([P, 2, E]), ALU.mult))
                then(dve.tensor_reduce(begin[:], jumps, AX_X, ALU.add))
                then(dve.scalar_tensor_tensor(begin[:], tile_f[:], float(P), begin[:], ALU.mult, ALU.add))
                then(dve.tensor_scalar(begin[:], begin[:], shift[:, 0:1], None, ALU.add))
                then(dve.tensor_scalar(expert[:], expert[:], float(E - 1), None, ALU.min))
                dve.tensor_scalar(table[:, 0, :], expert[:], float(2 * WEXP), None, ALU.mult)
                dve.tensor_copy(table[:, 1, :], expert[:])
                dve.tensor_scalar(table[:, 2, :], begin[:], float(SLOTS - P), None, ALU.min).then_inc(s_table, 1)

            dve.wait_ge(s_x[0], 16)
            normal(Item(0, 0, 2))
            normal_end(Item(0, 0, 2))
            dve.wait_ge(s_x[1], 16)
            normal(Item(0, 1, 2))
            normal_end(Item(0, 1, 2))
            dve.wait_ge(s_const, 18)
            dve.tensor_copy(tile_f[:], tile_i[:])
            dve.tensor_copy(token[:], token_i[:])
            dve.tensor_copy(first[:], first_i[:])
            dve.wait_ge(s_swhi, 1)
            dve.scalar_tensor_tensor(sw13[:, 1].rearrange("p w c n -> p (w c n)"), sw13_raw, W_UP,
                                     sw13[:, 0].rearrange("p w c n -> p (w c n)"), ALU.mult, ALU.subtract).then_inc(s_swlo, 1)
            route(Item(0, 0, 2))
            place(Item(0, 0, 2))
            for c in range(2, B):
                dve.wait_ge(s_x[c], 16)
            batch(Item(0, 0, 2))
            batch(Item(0, 1, 2))
            with dve.Fori(1, (B - 2) // 2) as r:
                for c in range(2):
                    batch(Item(r, c, 2))
            batch(Item(0, B - 2, 2), more=False)
            batch(Item(0, B - 1, 2), more=False, last=True)

            def low_rows(t):
                dve.wait_ge(s_eThi, t.n + 1)
                dve.scalar_tensor_tensor(xT[t.slot % 2][:, 1], chunks(ps[:, t.slot % 2, 0:H]), X_UP, xT[t.slot % 2][:, 0],
                                         ALU.mult, ALU.subtract).then_inc(s_eT, 1)

            def hidden_rows(t):
                dve.wait_ge(s_esilu, t.n + 1)
                if t.behind(2):
                    dve.wait_ge(s_ehT_ps, t.n - 1)
                dve.scalar_tensor_tensor(h_e[t.slot % 2], ps[:, 2 + t.slot % 2, I:2 * I], 1.0 / (X_UP * W_UP),
                                         silu_e[t.slot % 2], ALU.mult, ALU.mult).then_inc(s_eh, 1)

            def low_hidden(t):
                dve.wait_ge(s_ehThi, t.n + 1)
                dve.tensor_tensor(hT_e[t.slot % 2][:, 1], ps[:, 4 + t.slot % 2, 0:P], hT_e[t.slot % 2][:, 0],
                                  ALU.subtract).then_inc(s_ehT, 1)
            skewed(dve, SLOT_TILES, [(low_rows, 2), (hidden_rows, 1), (low_hidden, 0)])

            dve.wait_ge(s_xl, 16 * B)

            def sum_y(b):
                dve.wait_ge(s_fin[b.slot], b.rounds(16 * ACCS) + 16 * ACCS)
                a = [v[b.slot] for v in accs_l]
                for k in range(1, ACCS):
                    dve.tensor_tensor(a[0], a[0], a[k], ALU.add).then_inc(s_sum, 1)
                    if k < ACCS - 1:
                        dve.wait_ge(s_sum, b.n * (ACCS - 1) + k)

            def finish(b):
                dve.wait_ge(s_sg, b.n + 1)
                if b.behind(LAST_RING):
                    dve.wait_ge(s_out[b.slot], b.rounds(16))
                dve.tensor_tensor(o_l[b.slot], g_l[b.slot], x_last[:, bass.ds(b.n * (LT * H), LT * H)], ALU.add).then_inc(s_o, 1)
            sum_y(Item(0, 0, LAST_RING))

            def sum_and_finish(b):
                sum_y(Item(b.round, b.c + 1, LAST_RING))
                finish(b)
            for c in range(LAST_RING):
                sum_and_finish(Item(0, c, LAST_RING))
            with dve.Fori(1, LAST_ITEMS // LAST_RING - 1) as r:
                for c in range(LAST_RING):
                    sum_and_finish(Item(r, c, LAST_RING))
            for c in range(LAST_ITEMS - LAST_RING, LAST_ITEMS - 1):
                sum_and_finish(Item(0, c, LAST_RING))
            finish(Item(0, LAST_ITEMS - 1, LAST_RING))


def kernel(L0_attn_x, L0_attn_Wq, L0_attn_Wk, L0_attn_Wv, L0_attn_Wo, L0_ffn_gate_weight, L0_ffn_w1, L0_ffn_w2,
           L0_ffn_w3, L0_ffn_sw1, L0_ffn_sw2, L0_ffn_sw3):
    import concourse.bacc as bacc
    from concourse.bass_utils import run_bass_kernel_spmd as run

    def lay(a):
        return np.ascontiguousarray(a)

    a = {
        "x": lay(np.asarray(L0_attn_x).reshape(T, H)),
        "wq": lay(np.asarray(L0_attn_Wq)),
        "wk": lay(np.asarray(L0_attn_Wk)),
        "wvT": lay(np.asarray(L0_attn_Wv).T),
        "wo": lay(np.asarray(L0_attn_Wo)),
        "gwT": lay(np.asarray(L0_ffn_gate_weight).T),
    }
    w13 = np.stack([np.asarray(L0_ffn_w1), np.asarray(L0_ffn_w3)])
    w13 = w13.reshape(2, E, I, HC, P).transpose(4, 1, 3, 0, 2).reshape(P, E, HC * 2 * I)
    w2 = np.asarray(L0_ffn_w2).transpose(2, 0, 1)
    a["wexp"] = lay(np.concatenate([w13, w2], axis=2).reshape(P, E * WEXP))
    a["sw13T"] = lay(np.stack([np.asarray(L0_ffn_sw1).T, np.asarray(L0_ffn_sw3).T]))
    a["sw2T"] = lay(np.asarray(L0_ffn_sw2).T)

    nc = bacc.Bacc("TRN2", target_bir_lowering=False, num_devices=1)
    aps = [nc.dram_tensor(f"in_{n}", v.shape, mybir.dt.from_np(v.dtype), kind="ExternalInput").ap() for n, v in a.items()]
    out = nc.dram_tensor("out", (T, H), F32, kind="ExternalOutput").ap()
    gated_attention_moe(nc, *aps, out)
    r = run(nc, [{f"in_{n}": v for n, v in a.items()}], core_ids=[0])
    return r.results[0]["out"].reshape(B, S, H)
```
